# Optimizing a Trainium2 kernel written in Bass

```python
import numpy as np
import jax
import jax.numpy as jnp

def _softmax(x, axis=-1):
    return jax.nn.softmax(x, axis=axis)

def _gelu(x):
    return jax.nn.gelu(x, approximate=True)

def _silu(x):
    return jax.nn.silu(x)

def _sigmoid(x):
    return jax.nn.sigmoid(x)

def _layernorm(x, axis=-1, eps=1e-05):
    m = jnp.mean(x, axis=axis, keepdims=True)
    v = jnp.var(x, axis=axis, keepdims=True)
    return (x - m) / jnp.sqrt(v + eps)

def _scatter_add(tgt, idx, src, axis=0):
    return tgt.at[idx].add(src)

def _segment_sum(src, seg, n):
    return jax.ops.segment_sum(src, seg, n)
kernel_name = 'mk_seq_postln_d2_jaxref_r8_e5ca85'

def setup_inputs(seed: int=0):
    np.random.seed(seed)
    _w = jnp.asarray

    def _L0_attn_setup():
        import jax, jax.numpy as jnp
        import numpy as np
        key = jax.random.key(seed)
        x = jax.random.normal(key, (8, 96, 256), dtype=jnp.float32)
        return {'x': x}
    _L0_attn_in = _L0_attn_setup()

    def _L0_ffn_setup():
        import jax, jax.numpy as jnp
        import numpy as np
        BLOCK = 64

        def dequant4bit(q, scale):
            return (q.astype(jnp.float32) - 7.5) * jnp.repeat(scale, BLOCK, axis=1)
        key = jax.random.key(seed)
        ks = jax.random.split(key, 11)
        B, S, D, H, R = (4, 256, 256, 1024, 16)
        return {'x1': jax.random.normal(ks[0], (B, S, D), jnp.float32), 'w_up_q': jax.random.randint(ks[1], (H, D), 0, 16, dtype=jnp.int32), 'w_up_scale': jax.random.uniform(ks[2], (H, D // BLOCK), jnp.float32) * 0.02, 'b_up': jax.random.normal(ks[3], (H,), jnp.float32) * 0.01, 'w_up_lora_a': jax.random.normal(ks[4], (D, R), jnp.float32) * 0.02, 'w_up_lora_b': jax.random.normal(ks[5], (R, H), jnp.float32) * 0.02, 'w_down_q': jax.random.randint(ks[6], (D, H), 0, 16, dtype=jnp.int32), 'w_down_scale': jax.random.uniform(ks[7], (D, H // BLOCK), jnp.float32) * 0.02, 'b_down': jax.random.normal(ks[8], (D,), jnp.float32) * 0.01, 'w_down_lora_a': jax.random.normal(ks[9], (H, R), jnp.float32) * 0.02, 'w_down_lora_b': jax.random.normal(ks[10], (R, D), jnp.float32) * 0.02}
    _L0_ffn_in = _L0_ffn_setup()

    def _L1_attn_setup():
        import jax, jax.numpy as jnp
        import numpy as np
        D_ATTN = 256
        D_STATE = 64
        SHIFT_FRAC = 0.5
        LN_EPS = 1e-05

        def _reference_tuple_inner(x, W_key, W_value, W_output, W_shift, gate, time_decay, time_first, ln_gamma, ln_beta):
            B, T, D = x.shape
            shift_len = max(1, int(T * SHIFT_FRAC))
            x_cat = jnp.roll(x, -shift_len, axis=1)
            g = jax.nn.sigmoid(gate)
            x_shift = jnp.einsum('btd,ed->bte', x_cat, W_shift) * g + x * (1.0 - g)
            mu = jnp.mean(x_shift, axis=-1, keepdims=True)
            var = jnp.var(x_shift, axis=-1, keepdims=True)
            x_norm = (x_shift - mu) * jax.lax.rsqrt(var + LN_EPS) * ln_gamma + ln_beta
            k = jnp.einsum('btd,sd->bts', x_norm, W_key)
            v = jnp.einsum('btd,sd->bts', x_norm, W_value)
            w = jnp.exp(time_decay)
            u = jnp.exp(time_first)
            wkv = jnp.exp(-u * jax.nn.sigmoid(k)) * v

            def step(state, wkv_t):
                state = state * w + wkv_t
                return (state, state)
            init = jnp.zeros((B, k.shape[-1]), x.dtype)
            last_state, states = jax.lax.scan(step, init, jnp.swapaxes(wkv, 0, 1))
            states = jnp.swapaxes(states, 0, 1)
            output = jnp.einsum('bts,ds->btd', states, W_output)
            return (output, jax.lax.stop_gradient(last_state))
        key = jax.random.key(seed)
        ks = jax.random.split(key, 8)
        B, T = (8, 256)
        s_attn = 1.0 / np.sqrt(D_ATTN)
        s_state = 1.0 / np.sqrt(D_STATE)
        x = jax.random.normal(ks[0], (B, T, D_ATTN), jnp.float32)
        W_key = jax.random.normal(ks[1], (D_STATE, D_ATTN), jnp.float32) * s_attn
        W_value = jax.random.normal(ks[2], (D_STATE, D_ATTN), jnp.float32) * s_attn
        W_output = jax.random.normal(ks[3], (D_ATTN, D_STATE), jnp.float32) * s_state
        W_shift = jax.random.normal(ks[4], (D_ATTN, D_ATTN), jnp.float32) * s_attn
        gate = jnp.ones((D_ATTN,), jnp.float32)
        time_decay = -jax.random.uniform(ks[5], (D_STATE,), jnp.float32, 0.05, 1.0)
        time_first = jax.random.normal(ks[6], (D_STATE,), jnp.float32) * 0.1
        ln_gamma = jnp.ones((D_ATTN,), jnp.float32)
        ln_beta = jnp.zeros((D_ATTN,), jnp.float32)
        return dict(x=x, W_key=W_key, W_value=W_value, W_output=W_output, W_shift=W_shift, gate=gate, time_decay=time_decay, time_first=time_first, ln_gamma=ln_gamma, ln_beta=ln_beta)
    _L1_attn_in = _L1_attn_setup()

    def _L1_ffn_setup():
        import jax, jax.numpy as jnp
        import numpy as np
        K = 2

        def gelu(v):
            return jax.nn.gelu(v, approximate=False)
        key = jax.random.key(seed)
        ks = jax.random.split(key, 10)
        B, S, D, H, E = (4, 256, 256, 128, 8)
        SH = 2 * H
        u = lambda k_, shape, b: jax.random.uniform(k_, shape, jnp.float32, -b, b)
        return {'x': jax.random.normal(ks[0], (B, S, D), jnp.float32), 'gate_w': u(ks[1], (D, E), 1.0 / D), 'w1': u(ks[2], (E, D, H), 1.0 / D), 'b1': u(ks[3], (E, H), 1.0 / np.sqrt(D)), 'w2': u(ks[4], (E, H, D), 1.0 / H), 'b2': u(ks[5], (E, D), 1.0 / np.sqrt(H)), 'shared_w1': u(ks[6], (D, SH), 1.0 / D), 'shared_b1': u(ks[7], (SH,), 1.0 / np.sqrt(D)), 'shared_w2': u(ks[8], (SH, D), 1.0 / SH), 'shared_b2': u(ks[9], (D,), 1.0 / np.sqrt(SH))}
    _L1_ffn_in = _L1_ffn_setup()
    _d = {'L0_attn_x': _L0_attn_in['x'], 'L0_ffn_w_up_q': _L0_ffn_in['w_up_q'], 'L0_ffn_w_up_scale': _L0_ffn_in['w_up_scale'], 'L0_ffn_b_up': _L0_ffn_in['b_up'], 'L0_ffn_w_up_lora_a': _L0_ffn_in['w_up_lora_a'], 'L0_ffn_w_up_lora_b': _L0_ffn_in['w_up_lora_b'], 'L0_ffn_w_down_q': _L0_ffn_in['w_down_q'], 'L0_ffn_w_down_scale': _L0_ffn_in['w_down_scale'], 'L0_ffn_b_down': _L0_ffn_in['b_down'], 'L0_ffn_w_down_lora_a': _L0_ffn_in['w_down_lora_a'], 'L0_ffn_w_down_lora_b': _L0_ffn_in['w_down_lora_b'], 'L1_attn_W_key': _L1_attn_in['W_key'], 'L1_attn_W_value': _L1_attn_in['W_value'], 'L1_attn_W_output': _L1_attn_in['W_output'], 'L1_attn_W_shift': _L1_attn_in['W_shift'], 'L1_attn_gate': _L1_attn_in['gate'], 'L1_attn_time_decay': _L1_attn_in['time_decay'], 'L1_attn_time_first': _L1_attn_in['time_first'], 'L1_attn_ln_gamma': _L1_attn_in['ln_gamma'], 'L1_attn_ln_beta': _L1_attn_in['ln_beta'], 'L1_ffn_gate_w': _L1_ffn_in['gate_w'], 'L1_ffn_w1': _L1_ffn_in['w1'], 'L1_ffn_b1': _L1_ffn_in['b1'], 'L1_ffn_w2': _L1_ffn_in['w2'], 'L1_ffn_b2': _L1_ffn_in['b2'], 'L1_ffn_shared_w1': _L1_ffn_in['shared_w1'], 'L1_ffn_shared_b1': _L1_ffn_in['shared_b1'], 'L1_ffn_shared_w2': _L1_ffn_in['shared_w2'], 'L1_ffn_shared_b2': _L1_ffn_in['shared_b2']}
    _x0 = _d['L0_attn_x']
    _d['L0_attn_x'] = jax.random.normal(jax.random.fold_in(jax.random.key(seed), 1), (4, 512, 256), dtype=_x0.dtype)
    del _x0
    return _d

def reference(L0_attn_x, L0_ffn_w_up_q, L0_ffn_w_up_scale, L0_ffn_b_up, L0_ffn_w_up_lora_a, L0_ffn_w_up_lora_b, L0_ffn_w_down_q, L0_ffn_w_down_scale, L0_ffn_b_down, L0_ffn_w_down_lora_a, L0_ffn_w_down_lora_b, L1_attn_W_key, L1_attn_W_value, L1_attn_W_output, L1_attn_W_shift, L1_attn_gate, L1_attn_time_decay, L1_attn_time_first, L1_attn_ln_gamma, L1_attn_ln_beta, L1_ffn_gate_w, L1_ffn_w1, L1_ffn_b1, L1_ffn_w2, L1_ffn_b2, L1_ffn_shared_w1, L1_ffn_shared_b1, L1_ffn_shared_w2, L1_ffn_shared_b2):

    def _L0_attn_ref(x):
        import jax, jax.numpy as jnp
        import numpy as np
        energy = jnp.einsum('bci,bcj->bij', x, x)
        attention = jax.nn.softmax(energy, axis=-1)
        out = jnp.einsum('bcj,bij->bci', x, attention)
        return out

    def _L0_ffn_ref(x1, w_up_q, w_up_scale, b_up, w_up_lora_a, w_up_lora_b, w_down_q, w_down_scale, b_down, w_down_lora_a, w_down_lora_b):
        import jax, jax.numpy as jnp
        import numpy as np
        BLOCK = 64

        def dequant4bit(q, scale):
            return (q.astype(jnp.float32) - 7.5) * jnp.repeat(scale, BLOCK, axis=1)
        w_up = dequant4bit(w_up_q, w_up_scale).T
        y1 = x1 @ w_up + b_up + x1 @ w_up_lora_a @ w_up_lora_b
        x2 = jax.nn.relu(y1)
        w_down = dequant4bit(w_down_q, w_down_scale).T
        y2 = x2 @ w_down + b_down + x2 @ w_down_lora_a @ w_down_lora_b
        return y2

    def _L1_attn_ref(x, W_key, W_value, W_output, W_shift, gate, time_decay, time_first, ln_gamma, ln_beta):
        import jax, jax.numpy as jnp
        import numpy as np
        D_ATTN = 256
        D_STATE = 64
        SHIFT_FRAC = 0.5
        LN_EPS = 1e-05

        def _reference_tuple_inner(x, W_key, W_value, W_output, W_shift, gate, time_decay, time_first, ln_gamma, ln_beta):
            B, T, D = x.shape
            shift_len = max(1, int(T * SHIFT_FRAC))
            x_cat = jnp.roll(x, -shift_len, axis=1)
            g = jax.nn.sigmoid(gate)
            x_shift = jnp.einsum('btd,ed->bte', x_cat, W_shift) * g + x * (1.0 - g)
            mu = jnp.mean(x_shift, axis=-1, keepdims=True)
            var = jnp.var(x_shift, axis=-1, keepdims=True)
            x_norm = (x_shift - mu) * jax.lax.rsqrt(var + LN_EPS) * ln_gamma + ln_beta
            k = jnp.einsum('btd,sd->bts', x_norm, W_key)
            v = jnp.einsum('btd,sd->bts', x_norm, W_value)
            w = jnp.exp(time_decay)
            u = jnp.exp(time_first)
            wkv = jnp.exp(-u * jax.nn.sigmoid(k)) * v

            def step(state, wkv_t):
                state = state * w + wkv_t
                return (state, state)
            init = jnp.zeros((B, k.shape[-1]), x.dtype)
            last_state, states = jax.lax.scan(step, init, jnp.swapaxes(wkv, 0, 1))
            states = jnp.swapaxes(states, 0, 1)
            output = jnp.einsum('bts,ds->btd', states, W_output)
            return (output, jax.lax.stop_gradient(last_state))
        return _reference_tuple_inner(x, W_key, W_value, W_output, W_shift, gate, time_decay, time_first, ln_gamma, ln_beta)[0]

    def _L1_ffn_ref(x, gate_w, w1, b1, w2, b2, shared_w1, shared_b1, shared_w2, shared_b2):
        import jax, jax.numpy as jnp
        import numpy as np
        K = 2

        def gelu(v):
            return jax.nn.gelu(v, approximate=False)
        B, S, D = x.shape
        E = gate_w.shape[1]
        xf = x.reshape(-1, D)
        logits = xf @ gate_w
        top_logits, top_idx = jax.lax.top_k(logits, K)
        top_gates = jax.nn.softmax(top_logits, axis=-1)
        gates = jnp.sum(jax.nn.one_hot(top_idx, E, dtype=xf.dtype) * top_gates[..., None], axis=1)
        h = gelu(jnp.einsum('nd,edh->neh', xf, w1) + b1)
        out_e = jnp.einsum('neh,ehd->ned', h, w2) + b2
        routed = jnp.einsum('ne,ned->nd', gates, out_e)
        shared = gelu(xf @ shared_w1 + shared_b1) @ shared_w2 + shared_b2
        return (routed + shared).reshape(B, S, D)
    x = L0_attn_x
    x = _layernorm(x + _L0_attn_ref(x), axis=-1)
    x = _layernorm(x + _L0_ffn_ref(x, L0_ffn_w_up_q, L0_ffn_w_up_scale, L0_ffn_b_up, L0_ffn_w_up_lora_a, L0_ffn_w_up_lora_b, L0_ffn_w_down_q, L0_ffn_w_down_scale, L0_ffn_b_down, L0_ffn_w_down_lora_a, L0_ffn_w_down_lora_b), axis=-1)
    x = _layernorm(x + _L1_attn_ref(x, L1_attn_W_key, L1_attn_W_value, L1_attn_W_output, L1_attn_W_shift, L1_attn_gate, L1_attn_time_decay, L1_attn_time_first, L1_attn_ln_gamma, L1_attn_ln_beta), axis=-1)
    x = _layernorm(x + _L1_ffn_ref(x, L1_ffn_gate_w, L1_ffn_w1, L1_ffn_b1, L1_ffn_w2, L1_ffn_b2, L1_ffn_shared_w1, L1_ffn_shared_b1, L1_ffn_shared_w2, L1_ffn_shared_b2), axis=-1)
    return x

_drawn_inputs = setup_inputs


def setup_inputs(seed=0):
    import zlib

    import numpy as np

    out = dict(_drawn_inputs(seed))
    spreads = {'L1_attn_gate': (1.0, 0.2), 'L1_attn_ln_gamma': (1.0, 0.2), 'L1_attn_ln_beta': (0.0, 0.1)}
    factors = {'L0_ffn_b_up': 4.817,
     'L0_ffn_w_up_lora_a': 3.002,
     'L0_ffn_w_up_lora_b': 3.03,
     'L0_ffn_b_down': 4.889,
     'L1_ffn_w1': 8.0,
     'L1_ffn_b1': 8.0,
     'L1_ffn_w2': 8.0,
     'L1_ffn_shared_w1': 8.0,
     'L1_ffn_shared_b1': 8.0,
     'L1_ffn_shared_w2': 8.0}
    for name, (base, spread) in spreads.items():
        noise = np.random.default_rng([zlib.crc32(name.encode()), seed]).standard_normal(out[name].shape)
        drawn = base * np.exp(spread * noise) if base else spread * noise
        out[name] = jnp.asarray(drawn.astype(out[name].dtype))
    for name, factor in factors.items():
        out[name] = (out[name] * factor).astype(out[name].dtype)
    return out
```

```python
from contextlib import ExitStack

import concourse.bass as bass
from concourse import mybir

F32 = mybir.dt.float32
F32R = mybir.dt.float32r
I32 = mybir.dt.int32
ALU = mybir.AluOpType
ACT = mybir.ActivationFunctionType
AX = mybir.AxisListType

P = 128
EPS = 1e-5
BLOCK = 64
FILLER = -3.0e38
TAKEN = 3.0e38

LN_SUMS, LN_STATS, LN_AGGR, LN_DONE = 2, 6, 10, 14


def post_ln_kernel(nc, x, up_q, up_scale, b_up, up_a, up_b, dn_q, dn_scale, b_down, dn_a, dn_b,
                   w_key, w_value, w_output, w_shift, gate, time_decay, time_first, ln_gamma,
                   ln_beta, gate_w, w1, b1, w2, b2, sw1, sb1, sw2, sb2, out):
    B, T, D = x.shape
    H = up_q.shape[0]
    R = up_a.shape[1]
    S = w_key.shape[0]
    E = gate_w.shape[1]
    DT, TT, HT = D // P, T // P, H // P
    SHT = sw1.shape[1] // P
    NU = E + SHT
    assert (D, T, S, E, w1.shape[2], B) == (256, 512, 64, 8, P, 4)

    with ExitStack() as ctx:
        def sb(name, shape, dt=F32):
            return ctx.enter_context(nc.sbuf_tensor(name, shape, dt))

        def pair(name, shape):
            return sb(name + "_hi", shape, F32R), sb(name + "_lo", shape, F32R)

        def sem(name):
            return ctx.enter_context(nc.semaphore(name))

        def f32(ap):
            return ap.bitcast(F32)

        bank = {n: ctx.enter_context(nc.psum_tensor(n, [P, 512], F32))
                for n in ("T0", "T1", "U0", "U1", "D0", "D1", "M0", "M1")}
        Tb = [bank["T0"], bank["T1"]]
        Ub = [bank["U0"], bank["U1"]]
        Db = [bank["D0"], bank["D1"]]
        Mb = [bank["M0"], bank["M1"]]

        def tok(banks, t):
            return banks[t // 2][:, (t % 2) * D:(t % 2 + 1) * D]

        ident = sb("ident", [P, P])
        up_hl = pair("up_w", [P, DT, H])
        dn_hl = pair("dn_w", [P, HT, D])
        sh_hl = pair("shift_w", [P, DT, D])
        kv_hl = pair("kv_w", [P, DT, P])
        wo_hl = pair("out_w", [P, D])
        gw_hl = pair("gate_w", [P, DT, E])
        w1_hl = pair("w1_w", [P, E, DT, P])
        w2_hl = pair("w2_w", [P, E, D])
        sw1_hl = pair("sw1_w", [P, DT, SHT * P])
        sw2_hl = pair("sw2_w", [P, SHT, D])
        b2_hl = pair("b2_rows", [P, D])
        bup_c = sb("bup_c", [P, HT])
        b1_c = sb("b1_c", [P, NU])
        bdown_bc = sb("bdown_bc", [P, D])
        decay = sb("decay", [P, T])
        kvc = sb("kvc", [P, 4])
        stage_moe = sb("stage_moe", [P, E * T])
        stage_q = sb("stage_q", [P, HT * D + DT * H])
        stage_lora = sb("stage_lora", [P, 3 * H])
        stage_sw = sb("stage_sw", [P, 2 * T])

        def view(buf, at, *shape):
            n = shape[0] * (shape[1] if len(shape) > 1 else 1) * (shape[2] if len(shape) > 2 else 1)
            ap = buf[:, at:at + n]
            if len(shape) == 2:
                return ap.rearrange("p (a b) -> p a b", a=shape[0])
            if len(shape) == 3:
                return ap.rearrange("p (a b c) -> p a b c", a=shape[0], b=shape[1])
            return ap

        w1r = view(stage_moe, 0, E, DT, P)
        w2r = view(stage_moe, E * D, E, D)
        GB = 4
        gbc = view(stage_moe, 0, GB, T)
        x3_0 = view(stage_moe, GB * T, TT, D)
        x2keep = view(stage_moe, GB * T + TT * D, TT, D)
        z = x2keep
        wq = view(stage_q, 0, HT, D)
        wqd = view(stage_q, HT * D, DT, H)
        upq, dnq = wq.bitcast(I32), wqd.bitcast(I32)
        x2 = view(stage_q, 0, TT, D)
        x1 = view(stage_q, TT * D, TT, D)
        x1res = view(stage_q, 2 * TT * D, TT, D)
        rbuf = view(stage_q, 3 * TT * D, 2, T)
        upb = view(stage_lora, 0, H)
        dna = view(stage_lora, H, HT, P)
        dnaT = view(stage_lora, 2 * H, H)
        tanh_k = view(stage_lora, 0, T)
        ex_k = view(stage_lora, T, T)
        wkv = view(stage_lora, 2 * T, T)
        states = view(stage_lora, 3 * T, T)
        gbuf = view(stage_lora, 2 * H, 2, T)
        sw1r = view(stage_sw, 0, DT, SHT * P)
        sw2r = view(stage_sw, T, SHT, D)
        gAT = view(stage_sw, 0, T)
        gBT = view(stage_sw, T, T)
        ups = sb("ups", [P, HT, D // BLOCK])
        dns = sb("dns", [P, DT, H // BLOCK])
        obuf = sb("obuf", [P, TT, D])
        upa = obuf[:, 0, :].rearrange("p (t r) -> p t r", t=DT)
        dnb, upaT, gamma_bc = obuf[:, 1, :], obuf[:, 2, :], obuf[:, 3, :]
        gA = sb("gA", [P, TT, P])
        gB = sb("gB", [P, TT, P])
        shr = gA[:].rearrange("p t c -> p (t c)").rearrange("p (t d) -> p t d", t=DT)
        kvr = gB[:, 0:2, :].rearrange("p t c -> p (t c)")
        wor = gB[:, 2:4, :]
        gwr = sb("gwr", [P, DT, E])
        b2r = sb("b2r", [P, D])
        gate_bc = sb("gate_bc", [P, D])
        keep_bc = gate_bc
        gate_c = sb("gate_c", [P, 2 * DT])
        beta_bc = sb("beta_bc", [P, D])
        kvb = sb("kvb", [P, D])
        tdec = sb("tdec", [P, 2])
        mhalf = sb("mhalf", [P, TT])
        pad = sb("pad", [P, 1])
        xin = sb("xin", [P, TT, D])
        x_hl = pair("x_or_x2T", [P, TT * D])
        x2T_hl = [p[:].rearrange("p (t n) -> p t n", t=DT) for p in x_hl]
        x_hl = [p[:].rearrange("p (t n) -> p t n", t=TT) for p in x_hl]
        xT_hl = pair("xT_or_zT", [P, DT, T])
        zT_hl = xT_hl
        mx = sb("mx", [P, DT])
        nmx = sb("nmx", [P, DT])
        esum = sb("esum", [P, DT])
        erec = sb("erec", [P, DT])
        prob = sb("prob", [P, DT, D])
        PT_hl = pair("PT", [P, DT, D])
        x1T_hl = pair("x1T", [P, DT, T])
        st_hl = PT_hl[0][:].rearrange("p t d -> p (t d)")
        x3 = [x3_0, x1]
        x3T_hl = [pair("x3T", [P, DT, T]), x1T_hl]
        logit = sb("logit", [P, TT, 2 * E])
        top = sb("top", [P, TT, 8])
        marked = sb("marked", [P, TT, 2 * E])
        chosen = sb("chosen", [P, TT, E])
        gexp = sb("gexp", [P, TT, E])
        gsum = sb("gsum", [P, TT])
        gates = sb("gates", [P, TT, E])
        gates_hi = sb("gates_hi", [P, TT, E], F32R)
        gAT_r = sb("gAT_r", [P, T], F32R)
        r_hi = [sb(f"r_hi{i}", [P, T], F32R) for i in range(2)]
        r_lo = [sb(f"r_lo{i}", [P, T], F32R) for i in range(2)]
        ysum = sb("ysum", [P, TT, D])
        stats = sb("stats", [P, TT, 6])
        mv = {n: sb(f"mv{n}", [P, TT, 2]) for n in range(1, 6)}
        veps = sb("veps", [P, TT])
        rstd = {n: sb(f"rstd{n}", [P, TT]) for n in range(1, 6)}

        ld_x = sem("ld_x")
        ld_up = sem("ld_up")
        ld_dn = sem("ld_dn")
        ld_l1 = sem("ld_l1")
        ld_bc = sem("ld_bc")
        ld_moe = sem("ld_moe")
        saved = sem("saved")
        zeroed = sem("zeroed")
        id_ready = sem("id_ready")
        const_ready = sem("const_ready")
        fold_v = sem("fold_v")
        fold_a = sem("fold_a")
        lora_t = sem("lora_t")
        lora_sb = sem("lora_sb")
        up_ps = sem("up_ps")
        up_hi = sem("up_hi")
        up_lo = sem("up_lo")
        dn_ps = sem("dn_ps")
        dn_hi = sem("dn_hi")
        dn_lo = sem("dn_lo")
        l1_ps = sem("l1_ps")
        l1_hi = sem("l1_hi")
        l1_lo = sem("l1_lo")
        wsplit = sem("wsplit")
        t_ps = {n: sem(f"ps_{n}") for n in ("xT", "x1T", "x2T", "zT", "x3T")}
        t_hi = {n: sem(f"hi_{n}") for n in t_ps}
        t_lo = {n: sem(f"lo_{n}") for n in t_ps}
        ln = {n: sem(f"ln{n}") for n in range(1, 6)}
        ln_eps = {n: sem(f"ln_eps{n}") for n in range(1, 6)}
        ln_r = {n: sem(f"ln_rstd{n}") for n in range(1, 6)}
        x_parts = sem("x_parts")
        energy_ps = sem("energy_ps")
        soft_v = sem("soft_v")
        soft_e = sem("soft_e")
        PT_ps = sem("PT_ps")
        PT_hi = sem("PT_hi")
        PT_lo = sem("PT_lo")
        attn_ps = sem("attn_ps")
        res1 = sem("res1")
        hid_ps = sem("hid_ps")
        hid_r = sem("hid_r")
        hid_hi = sem("hid_hi")
        hid_lo = sem("hid_lo")
        ffn_ps = sem("ffn_ps")
        keep2 = sem("keep2")
        shift_ps = sem("shift_ps")
        kv_ps = sem("kv_ps")
        kv_act = sem("kv_act")
        kv_v = sem("kv_v")
        st_hi = sem("st_hi")
        out_ps = sem("out_ps")
        logit_ps = sem("logit_ps")
        gate_v = sem("gate_v")
        gate_e = sem("gate_e")
        gT_ps = sem("gT_ps")
        gT_sb = sem("gT_sb")
        g_bc = sem("g_bc")
        mhid_ps = sem("mhid_ps")
        mhid_r = sem("mhid_r")
        mhid_g = sem("mhid_g")
        mhid_hi = sem("mhid_hi")
        mhid_lo = sem("mhid_lo")
        moe_ps = sem("moe_ps")

        LN_OF = {1: (attn_ps, Mb), 2: (ffn_ps, Db), 3: (shift_ps, Mb), 4: (out_ps, Mb),
                 5: (moe_ps, Db)}
        N_GATE, N_SOFT, N_KV = 21, 5, 3

        L0 = [("x_split",), ("xT",), ("energy",), ("softmax",), ("PT",), ("attn",),
              ("ln_stats", 1), ("ln_apply", 1), ("x1T",)]
        L1 = [("x2T",), ("shift",), ("ln_stats", 3), ("ln_apply", 3), ("zT",), ("kv",), ("wkv",),
              ("outp",), ("ln_stats", 4), ("ln_apply", 4), ("x3T",), ("logits",), ("gating",),
              ("gT",)]
        FFN = [("up", 0), ("up", 1)]
        for k in range(HT):
            FFN += [("down", k)] + ([("up", k + 2)] if k + 2 < HT else [])
        FFN += [("ln_stats", 2), ("ln_apply", 2)]
        MOE = [("eup", 0), ("eup", 1), ("gbias",)]
        for k in range(NU):
            MOE += [("edown", k)] + ([("eup", k + 2)] if k + 2 < NU else [])
        MOE += [("ln_stats", 5), ("ln_apply", 5)]

        def of(b, steps):
            return [(s[0], b, *s[1:]) for s in steps]

        def woven(main, side, at):
            res = []
            for i, s in enumerate(main):
                res.append(s)
                res += [side[n] for n, a in enumerate(at) if a == i]
            return res

        AT_L1 = [1, 2, 4, 5, 6, 7, 8, 9, 10, 11, 13, 14, 15, 17]
        AT_L0 = [2, 3, 4, 5, 7, 10, 12, 13, 20]
        AT_L0_FFN = [1, 2, 3, 4, 6, 8, 10, 11, 15]
        AT_L1_MOE = [3, 4, 6, 7, 8, 10, 11, 12, 14, 15, 18, 19, 20, 22]

        PROLOGUE = (of(0, [("x_split",), ("xT",), ("energy",)]) + [("fold_up", 0)]
                    + of(0, [("softmax",), ("PT",), ("attn",), ("ln_stats", 1)])
                    + [("fold_down", 0)] + of(0, [("ln_apply", 1), ("x1T",)]) + [("fold_l1", 0)]
                    + woven(of(0, FFN), of(1, L0), AT_L0_FFN) + [("fold_moe", 0)])

        def middle(i):
            return (woven(of(i + 1, FFN), of(i, L1), AT_L1)
                    + woven(of(i, MOE), of(i + 2, L0), AT_L0))

        LAST = (woven(of(B - 1, FFN), of(B - 2, L1), AT_L1)
                + woven(of(B - 2, MOE), of(B - 1, L1), AT_L1_MOE) + of(B - 1, MOE))

        def slot(b):
            return 1 if isinstance(b, int) and b == B - 1 else 0

        def run(eng, ops):
            for s in PROLOGUE:
                if s[0] in ops:
                    ops[s[0]](*s[1:])
            for i in range(B - 2):
                for s in middle(i):
                    if s[0] in ops:
                        ops[s[0]](*s[1:])
            for s in LAST:
                if s[0] in ops:
                    ops[s[0]](*s[1:])

        block = ctx.enter_context(nc.Block())

        @block.sync
        def _(sp):
            def load_x(b):
                sp.dma_start(xin[:], x[b].rearrange("(t p) d -> p t d", p=P)).then_inc(ld_x, 16)

            load_x(0)
            sp.dma_start(upq, up_q.rearrange("(k p) d -> p k d", p=P)).then_inc(ld_up, 16)
            sp.dma_start(ups[:], up_scale.rearrange("(k p) c -> p k c", p=P)).then_inc(ld_up, 16)
            sp.wait_ge(zeroed, 1)
            sp.dma_start(upa[:, :, 0:R], up_a.rearrange("(t p) r -> p t r", p=P)).then_inc(ld_up, 16)
            sp.dma_start(upb[0:R, :], up_b).then_inc(ld_up, 16)
            sp.dma_start(bup_c[:], b_up.rearrange("(k p) -> p k", p=P),
                         allow_slow_non_contiguous=True).then_inc(ld_up, 16)
            sp.dma_start(dnq, dn_q.rearrange("(t p) h -> p t h", p=P)).then_inc(ld_dn, 16)
            sp.dma_start(dns[:], dn_scale.rearrange("(t p) c -> p t c", p=P)).then_inc(ld_dn, 16)
            sp.dma_start(dna[:, :, 0:R], dn_a.rearrange("(k p) r -> p k r", p=P)).then_inc(ld_dn, 16)
            sp.dma_start(dnb[0:R, :], dn_b).then_inc(ld_dn, 16)
            sp.dma_start(w1r, w1.rearrange("e (t p) h -> p e t h", p=P)).then_inc(ld_moe, 16)
            sp.dma_start(w2r, w2.rearrange("e p d -> p e d")).then_inc(ld_moe, 16)
            sp.dma_start(sw1r, sw1.rearrange("(t p) h -> p t h", p=P)).then_inc(ld_moe, 16)
            sp.dma_start(sw2r, sw2.rearrange("(t p) d -> p t d", p=P)).then_inc(ld_moe, 16)
            sp.dma_start(b2r[1:1 + E, :], b2).then_inc(ld_moe, 16)
            sp.dma_start(b2r[1 + E:1 + 2 * E, :], b2).then_inc(ld_moe, 16)
            sp.dma_start(b2r[1 + 2 * E:2 + 2 * E, :], sb2.rearrange("(a d) -> a d", a=1)).then_inc(ld_moe, 16)
            sp.dma_start(b1_c[:, 0:E], b1.rearrange("e p -> p e"),
                         allow_slow_non_contiguous=True).then_inc(ld_moe, 16)
            sp.dma_start(b1_c[:, E:NU], sb1.rearrange("(k p) -> p k", p=P),
                         allow_slow_non_contiguous=True).then_inc(ld_moe, 16)
            sp.dma_start(gwr[:], gate_w.rearrange("(t p) e -> p t e", p=P)).then_inc(ld_moe, 16)

            sp.wait_ge(ln[1], LN_SUMS)
            load_x(1)

            def save(b):
                sp.wait_ge(ln[5], b * LN_DONE + LN_DONE)
                sp.dma_start(out[b].rearrange("(t p) d -> p t d", p=P), obuf[:]).then_inc(saved, 16)

            for i in range(B - 2):
                sp.wait_ge(ln[1], (i + 1) * LN_DONE + LN_SUMS)
                sp.dma_start(xin[:], x.rearrange("b (t p) d -> b p t d", p=P)[bass.ds(i + 2, 1)].rearrange("a p t d -> (a p) t d")).then_inc(ld_x, 16)
                sp.wait_ge(ln[5], i * LN_DONE + LN_DONE)
                sp.dma_start(out.rearrange("b (t p) d -> b p t d", p=P)[bass.ds(i, 1)].rearrange("a p t d -> (a p) t d"), obuf[:]).then_inc(saved, 16)
            for b in (B - 2, B - 1):
                save(b)
            sp.wait_ge(saved, 16 * (B + 1))

        @block.gpsimd
        def _(pool):
            g = nc.gpsimd
            g.memset(upa, 0.0)
            g.memset(upb, 0.0)
            g.memset(dna, 0.0)
            g.memset(dnb, 0.0)
            g.memset(b2r[:], 0.0).then_inc(zeroed, 1)
            g.memset(ident[:], 0.0).then_inc(id_ready, 1)
            pool.wait_ge(id_ready, 1)
            g.affine_select(out=ident[:], in_=ident[:], compare_op=ALU.not_equal, fill=1.0, base=0,
                            pattern=[[-1, P]], channel_multiplier=1).then_inc(id_ready, 1)
            g.memset(mhalf[:], -0.5).then_inc(const_ready, 1)
            g.memset(logit[:], FILLER).then_inc(const_ready, 1)

            def x_split(b):
                pool.wait_ge(ld_x, b * 16 + 16)
                if not (isinstance(b, int) and b < 2):
                    pool.wait_ge(shift_ps, (b - 2) * 2 + 2)
                g.tensor_copy(x_hl[0][:], xin[:]).then_inc(x_parts, 1)
                pool.wait_ge(x_parts, b * 2 + 1)
                g.tensor_tensor(x_hl[1][:], xin[:], f32(x_hl[0][:]), ALU.subtract).then_inc(x_parts, 1)

            def ln_stats(b, n):
                if n == 1:
                    pool.wait_ge(const_ready, 3)
                pool.wait_ge(ln[n], b * LN_DONE + LN_AGGR)
                g.tensor_scalar(veps[:], mv[n][:, :, 1], EPS, None, ALU.add).then_inc(ln_eps[n], 1)
                pool.wait_ge(ln_eps[n], b + 1)
                g.tensor_tensor(rstd[n][:], veps[:], mhalf[:], ALU.pow).then_inc(ln_r[n], 1)

            def bias_row(b):
                pool.wait_ge(ld_bc, 16 * 5)
                if isinstance(b, int) and b == 0:
                    pool.wait_ge(dn_lo, 4)
                else:
                    pool.wait_ge(ln[2], (b - 1) * LN_DONE + LN_SUMS)
                pool.wait_ge(ln[1], b * LN_DONE + LN_DONE)
                for t in range(TT):
                    op = g.tensor_tensor(x1res[:, t, :], x1[:, t, :], bdown_bc[:], ALU.add)
                    op.then_inc(res1, 1)

            def keep_row(b):
                pool.wait_ge(fold_a, 3)
                pool.wait_ge(fold_v, 8)
                pool.wait_ge(ln[2], b * LN_DONE + LN_DONE)
                for t in range(TT):
                    g.tensor_tensor(x2keep[:, t, :], x2[:, t, :], keep_bc[:], ALU.mult).then_inc(keep2, 1)

            def fold_moe(_):
                pool.wait_ge(ld_moe, 16 * 10)
                parts = [(gw_hl, gwr), (b2_hl, b2r), (w1_hl, w1r), (w2_hl, w2r), (sw1_hl, sw1r),
                         (sw2_hl, sw2r)]
                for n, (hl, raw) in enumerate(parts):
                    g.tensor_copy(hl[0][:], raw[:]).then_inc(wsplit, 1)
                    pool.wait_ge(wsplit, 2 * n + 1)
                    g.tensor_tensor(hl[1][:], raw[:], f32(hl[0][:]), ALU.subtract).then_inc(wsplit, 1)

            def fold_l1(_):
                pool.wait_ge(l1_ps, 2)
                g.memset(gA[:], 0.0).then_inc(const_ready, 1)
                pool.wait_ge(const_ready, 4)
                g.memset(gA[:, :, 1 + 2 * E:2 + 2 * E], 1.0).then_inc(const_ready, 1)
                g.memset(gB[:], 0.0).then_inc(const_ready, 1)

            def gT(b):
                pool.wait_ge(gT_sb, b * 3 + 1)
                for e in range(GB):
                    g.drain()
                    g.partition_broadcast(gbc[:, e, :], gAT[32 * e:32 * e + 1, :],
                                          channels=P).then_inc(g_bc, 1)
                g.drain()

            def eup(b, k):
                if k + GB < E:
                    pool.wait_ge(gT_sb, b * 3 + 2)
                    pool.wait_ge(mhid_g, b * E + k + 1)
                    g.drain()
                    g.partition_broadcast(gbc[:, k, :], gBT[32 * k:32 * k + 1, :],
                                          channels=P).then_inc(g_bc, 1)
                    g.drain()

            def ln_apply(b, n):
                if n == 1:
                    bias_row(b)
                if n == 2:
                    keep_row(b)

            run(pool, {"x_split": x_split, "ln_stats": ln_stats, "ln_apply": ln_apply, "gT": gT,
                       "eup": eup, "fold_down": fold_moe, "fold_l1": fold_l1})

        @block.scalar
        def _(act):
            a = nc.scalar
            for dst, src in ((bdown_bc, b_down), (gate_bc, gate), (gamma_bc, ln_gamma),
                             (beta_bc, ln_beta)):
                act.dma_start(dst[:], src.rearrange("(a d) -> a d", a=1).to_broadcast((P, D))).then_inc(ld_bc, 16)
            act.dma_start(gate_c[:, 0:DT], gate.rearrange("(t p) -> p t", p=P),
                          allow_slow_non_contiguous=True).then_inc(ld_bc, 16)
            act.dma_start(shr[:], w_shift.rearrange("(t p) d -> p t d", p=P)).then_inc(ld_l1, 16)
            act.dma_start(kvr[0:S, :], w_value).then_inc(ld_l1, 16)
            act.dma_start(kvr[S:2 * S, :], w_key).then_inc(ld_l1, 16)
            act.dma_start(wor[:, :, 0:S], w_output.rearrange("(t p) s -> p t s", p=P)).then_inc(ld_l1, 16)
            act.dma_start(wor[:, :, S:2 * S], w_output.rearrange("(t p) s -> p t s", p=P)).then_inc(ld_l1, 16)
            act.dma_start(tdec[0:S, 0:1], time_decay.rearrange("(s a) -> s a", a=1)).then_inc(ld_l1, 16)
            act.dma_start(tdec[S:2 * S, 0:1], time_first.rearrange("(s a) -> s a", a=1)).then_inc(ld_l1, 16)

            def turned(name, hl, b):
                for t in range(DT):
                    act.wait_ge(t_ps[name], b * DT + t + 1)
                    a.activation(hl[0][:, t, :], Tb[t][:], ACT.Copy).then_inc(t_hi[name], 1)

            def softmax(b):
                act.wait_ge(soft_v, b * N_SOFT + 2)
                for i in range(DT):
                    a.activation(prob[:, i, :], Mb[0][:, i * D:(i + 1) * D], ACT.Exp, bias=nmx[:, i:i + 1],
                                 accum_out=esum[:, i:i + 1]).then_inc(soft_e, 1)

            def PT(b):
                act.wait_ge(PT_ps, b + 1)
                a.activation(PT_hl[0][:].rearrange("p t d -> p (t d)"), Mb[1][:], ACT.Copy).then_inc(PT_hi, 1)

            def fold_up(_):
                act.wait_ge(lora_t, 1)
                a.activation(upaT[:], Db[1][:, 0:D], ACT.Copy).then_inc(lora_sb, 1)
                for i in range(2):
                    act.wait_ge(lora_t, 2 + i)
                    a.activation(dnaT[:, i * 512:(i + 1) * 512], Ub[i][:], ACT.Copy).then_inc(lora_sb, 1)
                for n in range(4):
                    act.wait_ge(up_ps, n + 1)
                    a.activation(up_hl[0][:, n // 2, (n % 2) * 512:(n % 2 + 1) * 512], (Db + Ub)[n][:],
                                 ACT.Copy).then_inc(up_hi, 1)

            def fold_down(_):
                for n in range(4):
                    act.wait_ge(dn_ps, n + 1)
                    a.activation(dn_hl[0][:, 2 * n:2 * n + 2, :].rearrange("p k d -> p (k d)"),
                                 (Db + Ub)[n][:], ACT.Copy).then_inc(dn_hi, 1)
                act.wait_ge(ld_bc, 16 * 5)
                a.activation(gate_bc[:], gate_bc[:], ACT.Tanh, scale=0.5).then_inc(fold_a, 1)
                a.activation(gate_c[:, DT:2 * DT], gate_c[:, 0:DT], ACT.Tanh, scale=0.5).then_inc(fold_a, 1)
                act.wait_ge(ld_l1, 16 * 7)
                a.activation(tdec[:, 1:2], tdec[:, 0:1], ACT.Exp).then_inc(fold_a, 1)

            def fold_l1(_):
                act.wait_ge(l1_ps, 1)
                a.activation(sh_hl[0][:].rearrange("p t d -> p (t d)"), Mb[0][:], ACT.Copy).then_inc(l1_hi, 1)
                act.wait_ge(l1_ps, 2)
                a.activation(kv_hl[0][:].rearrange("p t d -> p (t d)"), Mb[1][:, 0:D], ACT.Copy).then_inc(l1_hi, 1)
                a.activation(wo_hl[0][:], Mb[1][:, D:2 * D], ACT.Copy).then_inc(l1_hi, 1)

            def up(b, k):
                act.wait_ge(hid_ps, b * HT + k + 1)
                a.activation(rbuf[:, k % 2, :], Ub[k % 2][:], ACT.Relu, bias=bup_c[:, k:k + 1]).then_inc(hid_r, 1)
                act.wait_ge(hid_r, b * HT + k + 1)
                a.activation(r_hi[k % 2][:], rbuf[:, k % 2, :], ACT.Copy).then_inc(hid_hi, 1)

            def kv(b):
                act.wait_ge(kv_ps, b + 1)
                a.activation(tanh_k[S:2 * S, :], Mb[0][S:2 * S, :], ACT.Tanh, bias=kvc[S:2 * S, 1:2],
                             scale=0.5).then_inc(kv_act, 1)
                act.wait_ge(kv_act, b * 2 + 1)
                a.activation(ex_k[0:S, :], tanh_k[S:2 * S, :], ACT.Exp, bias=kvc[S:2 * S, 2:3],
                             scale=kvc[S:2 * S, 2:3]).then_inc(kv_act, 1)

            def states_hi(b):
                act.wait_ge(kv_v, b * N_KV + 2)
                a.activation(st_hl[0:S, :], states[0:S, :], ACT.Copy).then_inc(st_hi, 1)

            def gating(b):
                act.wait_ge(gate_v, b * N_GATE + 11)
                a.activation(gexp[:], gexp[:], ACT.Exp).then_inc(gate_e, 1)

            def gT(b):
                act.wait_ge(gT_ps, b * 2 + 1)
                a.activation(gAT, Tb[0][:], ACT.Copy).then_inc(gT_sb, 1)
                act.wait_ge(gT_ps, b * 2 + 2)
                a.activation(gBT, Tb[1][:], ACT.Copy).then_inc(gT_sb, 1)
                a.activation(gAT_r[:], Tb[0][:], ACT.Copy).then_inc(gT_sb, 1)

            def eup(b, k):
                act.wait_ge(mhid_ps, b * NU + k + 1)
                a.activation(rbuf[:, k % 2, :], Ub[k % 2][:], ACT.Gelu, bias=b1_c[:, k:k + 1]).then_inc(mhid_r, 1)
                if k < E:
                    act.wait_ge(mhid_g, b * E + k + 1)
                    src = gbuf
                else:
                    act.wait_ge(mhid_r, b * NU + k + 1)
                    src = rbuf
                a.activation(r_hi[k % 2][:], src[:, k % 2, :], ACT.Copy).then_inc(mhid_hi, 1)

            run(act, {
                "xT": lambda b: turned("xT", xT_hl, b), "x1T": lambda b: turned("x1T", x1T_hl, b),
                "x2T": lambda b: turned("x2T", x2T_hl, b), "zT": lambda b: turned("zT", zT_hl, b),
                "x3T": lambda b: turned("x3T", x3T_hl[slot(b)], b), "softmax": softmax, "PT": PT,
                "fold_up": fold_up, "fold_down": fold_down, "fold_l1": fold_l1, "up": up, "kv": kv,
                "wkv": states_hi, "gating": gating, "gT": gT, "eup": eup})

        @block.vector
        def _(dve):
            v = nc.vector
            v.memset(pad[:], 0.0).then_inc(saved, 16)
            v.memset(decay[:], 1.0).then_inc(const_ready, 1)

            def turned(name, hl, b):
                for t in range(DT):
                    dve.wait_ge(t_hi[name], b * DT + t + 1)
                    v.tensor_tensor(hl[1][:, t, :], Tb[t][:], f32(hl[0][:, t, :]), ALU.subtract).then_inc(t_lo[name], 1)

            def ln_stats(b, n):
                ready, banks = LN_OF[n]
                res = {1: xin, 2: x1res, 3: x2keep, 4: x2, 5: x3[slot(b)]}[n]
                base = b * LN_DONE
                if n == 2:
                    dve.wait_ge(res1, b * TT + TT)
                if n == 3:
                    dve.wait_ge(keep2, b * TT + TT)
                for i in range(2):
                    dve.wait_ge(ready, b * 2 + i + 1)
                    v.tensor_tensor(ysum[:, 2 * i:2 * i + 2, :].rearrange("p t d -> p (t d)"), banks[i][:],
                                    res[:, 2 * i:2 * i + 2, :].rearrange("p t d -> p (t d)"),
                                    ALU.add).then_inc(ln[n], 1)
                for t in range(TT):
                    dve.wait_ge(ln[n], base + t // 2 + 1 if t < 2 else base + LN_SUMS + t - 2 + (0 if t == 2 else 0))
                    v.bn_stats(stats[:, t, :], ysum[:, t, :]).then_inc(ln[n], 1)
                for t in range(TT):
                    dve.wait_ge(ln[n], base + LN_SUMS + TT)
                    v.bn_aggr(mv[n][:, t, :], stats[:, t, :]).then_inc(ln[n], 1)

            def ln_apply(b, n):
                dst = {1: x1, 2: x2, 3: z, 4: x3[slot(b)], 5: obuf}[n]
                if n == 5:
                    dve.wait_ge(saved, b * 16 + 16)
                dve.wait_ge(ln_r[n], b + 1)
                for t in range(TT):
                    v.tensor_scalar(dst[:, t, :], ysum[:, t, :], mv[n][:, t, 0:1], rstd[n][:, t:t + 1],
                                    ALU.subtract, ALU.mult).then_inc(ln[n], 1)

            def softmax(b):
                base = b * N_SOFT
                dve.wait_ge(energy_ps, b + 1)
                v.tensor_reduce(mx[:], Mb[0][:].rearrange("p (i j) -> p i j", i=DT), AX.X, ALU.max).then_inc(soft_v, 1)
                dve.wait_ge(soft_v, base + 1)
                v.tensor_scalar(nmx[:], mx[:], -1.0, None, ALU.mult).then_inc(soft_v, 1)
                dve.wait_ge(soft_e, b * DT + DT)
                v.reciprocal(erec[:], esum[:]).then_inc(soft_v, 1)
                dve.wait_ge(soft_v, base + 3)
                for i in range(DT):
                    v.tensor_scalar(prob[:, i, :], prob[:, i, :], erec[:, i:i + 1], None, ALU.mult).then_inc(soft_v, 1)

            def PT(b):
                dve.wait_ge(PT_hi, b + 1)
                v.tensor_tensor(PT_hl[1][:].rearrange("p t d -> p (t d)"), Mb[1][:],
                                f32(PT_hl[0][:]).rearrange("p t d -> p (t d)"), ALU.subtract).then_inc(PT_lo, 1)

            def dequant(dst, q, scale, n):
                v.scalar_tensor_tensor(
                    out=dst.rearrange("p k (c j) -> p (k c) j", j=BLOCK),
                    in0=q.rearrange("p k (c j) -> p (k c) j", j=BLOCK), scalar=-7.5,
                    in1=scale[:].rearrange("p k (c a) -> p (k c) a", a=1).to_broadcast((P, n, BLOCK)),
                    op0=ALU.add, op1=ALU.mult).then_inc(fold_v, 1)

            def fold_up(_):
                dve.wait_ge(ld_up, 16 * 5)
                dequant(wq, upq, ups, HT * D // BLOCK)
                for n in range(4):
                    dst = (slice(None), n // 2, slice((n % 2) * 512, (n % 2 + 1) * 512))
                    dve.wait_ge(up_hi, n + 1)
                    v.tensor_tensor(up_hl[1][dst], (Db + Ub)[n][:], f32(up_hl[0][dst]), ALU.subtract).then_inc(up_lo, 1)

            def fold_down(_):
                dve.wait_ge(ld_dn, 16 * 4)
                dequant(wqd, dnq, dns, DT * H // BLOCK)
                for n in range(4):
                    dve.wait_ge(dn_hi, n + 1)
                    v.tensor_tensor(dn_hl[1][:, 2 * n:2 * n + 2, :].rearrange("p k d -> p (k d)"), (Db + Ub)[n][:],
                                    f32(dn_hl[0][:, 2 * n:2 * n + 2, :]).rearrange("p k d -> p (k d)"),
                                    ALU.subtract).then_inc(dn_lo, 1)
                dve.wait_ge(fold_a, 2)
                v.tensor_scalar(gate_c[:, 0:DT], gate_c[:, DT:2 * DT], 0.5, 0.5, ALU.mult, ALU.add).then_inc(fold_v, 1)
                v.tensor_scalar(keep_bc[:], gate_bc[:], -0.5, 0.5, ALU.mult, ALU.add).then_inc(fold_v, 1)
                dve.wait_ge(ld_l1, 16 * 7)
                dve.wait_ge(fold_v, 4)
                for t in range(DT):
                    v.tensor_scalar(shr[:, t, :], shr[:, t, :], gate_c[:, t:t + 1], None, ALU.mult).then_inc(fold_v, 1)
                v.tensor_tensor(kvb[:], kvr[:], beta_bc[:], ALU.mult).then_inc(fold_v, 1)
                v.tensor_tensor(kvr[:], kvr[:], gamma_bc[:], ALU.mult).then_inc(fold_v, 1)
                dve.wait_ge(fold_v, 8)
                v.tensor_reduce(kvc[:, 0:1], kvb[:], AX.X, ALU.add).then_inc(fold_v, 1)
                dve.wait_ge(fold_v, 9)
                v.tensor_scalar(kvc[:, 1:2], kvc[:, 0:1], 0.5, None, ALU.mult).then_inc(fold_v, 1)
                dve.wait_ge(fold_a, 3)
                v.tensor_scalar(kvc[:, 2:3], tdec[:, 1:2], -0.5, None, ALU.mult).then_inc(fold_v, 1)
                dve.wait_ge(const_ready, 3)
                v.tensor_scalar(decay[0:S, :], decay[0:S, :], tdec[0:S, 1:2], None, ALU.mult).then_inc(fold_v, 1)

            def fold_l1(_):
                dve.wait_ge(l1_hi, 1)
                v.tensor_tensor(sh_hl[1][:].rearrange("p t d -> p (t d)"), Mb[0][:],
                                f32(sh_hl[0][:]).rearrange("p t d -> p (t d)"), ALU.subtract).then_inc(l1_lo, 1)
                dve.wait_ge(l1_hi, 3)
                v.tensor_tensor(kv_hl[1][:].rearrange("p t d -> p (t d)"), Mb[1][:, 0:D],
                                f32(kv_hl[0][:]).rearrange("p t d -> p (t d)"), ALU.subtract).then_inc(l1_lo, 1)
                v.tensor_tensor(wo_hl[1][:], Mb[1][:, D:2 * D], f32(wo_hl[0][:]), ALU.subtract).then_inc(l1_lo, 1)

            def up(b, k):
                dve.wait_ge(hid_hi, b * HT + k + 1)
                v.tensor_tensor(r_lo[k % 2][:], rbuf[:, k % 2, :], f32(r_hi[k % 2][:]), ALU.subtract).then_inc(hid_lo, 1)

            def recur(b):
                dve.wait_ge(kv_act, b * 2 + 2)
                if isinstance(b, int) and b == 0 or True:
                    dve.wait_ge(fold_v, 12)
                v.scalar_tensor_tensor(out=wkv[0:S, :], in0=Mb[0][0:S, :], scalar=kvc[0:S, 0:1],
                                       in1=ex_k[0:S, :], op0=ALU.add, op1=ALU.mult).then_inc(kv_v, 1)
                dve.wait_ge(kv_v, b * N_KV + 1)
                v.tensor_tensor_scan(states[0:S, :], decay[0:S, :], wkv[0:S, :], 0.0, ALU.mult, ALU.add).then_inc(kv_v, 1)
                dve.wait_ge(st_hi, b + 1)
                v.tensor_tensor(st_hl[S:2 * S, :], states[0:S, :], f32(st_hl[0:S, :]), ALU.subtract).then_inc(kv_v, 1)

            def gating(b):
                base, n = b * N_GATE, [0]

                def step(op):
                    op.then_inc(gate_v, 1)
                    n[0] += 1

                def settle():
                    dve.wait_ge(gate_v, base + n[0])

                dve.wait_ge(logit_ps, b + 1)
                dve.wait_ge(const_ready, 6)
                step(v.tensor_copy(logit[:, :, 0:E], Mb[1][:, 0:TT * E].rearrange("p (t e) -> p t e", t=TT)))
                settle()
                for t in range(TT):
                    step(v.max(top[:, t, :], logit[:, t, :]))
                settle()
                step(v.tensor_tensor(gexp[:], logit[:, :, 0:E], top[:, :, 0:1].to_broadcast((P, TT, E)), ALU.subtract))
                step(v.memset(top[:, :, 2:8], FILLER))
                settle()
                for t in range(TT):
                    step(v.match_replace(marked[:, t, :], top[:, t, :], logit[:, t, :], TAKEN))
                settle()
                step(v.tensor_scalar(chosen[:], marked[:, :, 0:E], TAKEN, None, ALU.is_equal))
                dve.wait_ge(gate_e, b + 1)
                settle()
                step(v.tensor_tensor(gates[:], gexp[:], chosen[:], ALU.mult))
                settle()
                step(v.tensor_reduce(gsum[:], gates[:], AX.X, ALU.add))
                settle()
                step(v.reciprocal(gsum[:], gsum[:]))
                settle()
                step(v.tensor_tensor(gates[:], gates[:], gsum[:].rearrange("p (t a) -> p t a", a=1).to_broadcast((P, TT, E)), ALU.mult))
                settle()
                step(v.tensor_copy(gates_hi[:], gates[:]))
                step(v.tensor_copy(gA[:].rearrange("p t (j c) -> p t j c", c=32)[:, :, :, 0], gates[:, :, 0:4]))
                step(v.tensor_copy(gB[:].rearrange("p t (j c) -> p t j c", c=32)[:, :, :, 0], gates[:, :, 4:8]))
                settle()
                step(v.tensor_copy(gA[:, :, 1:1 + E], f32(gates_hi[:])))
                step(v.tensor_tensor(gA[:, :, 1 + E:1 + 2 * E], gates[:], f32(gates_hi[:]), ALU.subtract))
                while n[0] < N_GATE:
                    step(v.memset(pad[:], 0.0))

            def eup(b, k):
                src = rbuf
                if k < E:
                    dve.wait_ge(mhid_r, b * NU + k + 1)
                    dve.wait_ge(g_bc, b * E + k + 1)
                    v.tensor_tensor(gbuf[:, k % 2, :], rbuf[:, k % 2, :], gbc[:, k % GB, :], ALU.mult).then_inc(mhid_g, 1)
                    src = gbuf
                dve.wait_ge(mhid_hi, b * NU + k + 1)
                v.tensor_tensor(r_lo[k % 2][:], src[:, k % 2, :], f32(r_hi[k % 2][:]), ALU.subtract).then_inc(mhid_lo, 1)

            run(dve, {
                "xT": lambda b: turned("xT", xT_hl, b), "x1T": lambda b: turned("x1T", x1T_hl, b),
                "x2T": lambda b: turned("x2T", x2T_hl, b), "zT": lambda b: turned("zT", zT_hl, b),
                "x3T": lambda b: turned("x3T", x3T_hl[slot(b)], b), "softmax": softmax, "PT": PT,
                "ln_stats": ln_stats, "ln_apply": ln_apply, "fold_up": fold_up, "fold_down": fold_down,
                "fold_l1": fold_l1, "up": up, "wkv": recur, "gating": gating, "eup": eup})

        @block.tensor
        def _(pe):
            mm = nc.tensor.matmul

            def three(dst, w_hl, m_hl, cols, rows, first, last):
                for i, (w, m) in enumerate(((0, 0), (0, 1), (1, 0))):
                    op = mm(dst, w_hl[w][cols], m_hl[m][rows], start=first and i == 0,
                            stop=last and i == 2, skip_group_check=True)
                return op

            def turn(src, name, after, b, count):
                for t in range(DT):
                    for c in range(TT):
                        if t == 0:
                            pe.wait_ge(after, b * count + count - TT + c + 1)
                        op = nc.tensor.transpose(Tb[t][:, c * P:(c + 1) * P], src[:, c, t * P:(t + 1) * P], ident[:])
                    op.then_inc(t_ps[name], 1)

            def xT(b):
                pe.wait_ge(id_ready, 2)
                pe.wait_ge(ld_x, b * 16 + 16)
                for t in range(DT):
                    for c in range(TT):
                        op = nc.tensor.transpose(Tb[t][:, c * P:(c + 1) * P], xin[:, c, t * P:(t + 1) * P], ident[:])
                    op.then_inc(t_ps["xT"], 1)

            def energy(b):
                pe.wait_ge(x_parts, b * 2 + 2)
                for i in range(DT):
                    for c in range(TT):
                        op = three(Mb[0][:, i * D:(i + 1) * D], x_hl, x_hl, (slice(None), c, slice(i * P, (i + 1) * P)),
                                   (slice(None), c, slice(None)), c == 0, c == TT - 1)
                op.then_inc(energy_ps, 1)

            def PT(b):
                pe.wait_ge(soft_v, b * N_SOFT + 5)
                for j in range(DT):
                    for i in range(DT):
                        op = nc.tensor.transpose(Mb[1][:, j * D + i * P:j * D + (i + 1) * P],
                                                 prob[:, i, j * P:(j + 1) * P], ident[:])
                op.then_inc(PT_ps, 1)

            def attn(b):
                pe.wait_ge(PT_lo, b + 1)
                pe.wait_ge(t_lo["xT"], b * DT + DT)
                for c in range(TT):
                    for j in range(DT):
                        op = three(tok(Mb, c), xT_hl, PT_hl, (slice(None), j, slice(c * P, (c + 1) * P)),
                                   (slice(None), j, slice(None)), j == 0, j == DT - 1)
                    if c % 2:
                        op.then_inc(attn_ps, 1)

            def fold_up(_):
                pe.wait_ge(ld_up, 16 * 5)
                for t in range(DT):
                    op = nc.tensor.transpose(Db[1][:, t * P:(t + 1) * P], upa[:, t, :], ident[:])
                op.then_inc(lora_t, 1)
                pe.wait_ge(ld_dn, 16 * 4)
                for k in range(HT):
                    op = nc.tensor.transpose(Ub[k // 4][:, k % 4 * P:(k % 4 + 1) * P], dna[:, k, :], ident[:])
                    if k % 4 == 3:
                        op.then_inc(lora_t, 1)
                pe.wait_ge(lora_sb, 3)
                pe.wait_ge(fold_v, 1)
                for n in range(4):
                    t, half = n // 2, n % 2
                    dst = (Db + Ub)[n]
                    mm(dst[:], upaT[:, t * P:(t + 1) * P], upb[:, half * 512:(half + 1) * 512], start=True,
                       stop=False, skip_group_check=True)
                    for k in range(4):
                        op = mm(dst[:, k * P:(k + 1) * P], wq[:, half * 4 + k, t * P:(t + 1) * P], ident[:],
                                start=False, stop=True, skip_group_check=True)
                    op.then_inc(up_ps, 1)

            def fold_down(_):
                pe.wait_ge(fold_v, 2)
                for n in range(4):
                    pe.wait_ge(up_lo, n + 1)
                    dst = (Db + Ub)[n]
                    for k in range(2):
                        cols = slice(k * D, (k + 1) * D)
                        mm(dst[:, cols], dnaT[:, (2 * n + k) * P:(2 * n + k + 1) * P], dnb, start=k == 0,
                           stop=False, skip_group_check=True)
                    for k in range(2):
                        for t in range(DT):
                            op = mm(dst[:, k * D + t * P:k * D + (t + 1) * P], wqd[:, t, (2 * n + k) * P:(2 * n + k + 1) * P],
                                    ident[:], start=False, stop=True, skip_group_check=True)
                    op.then_inc(dn_ps, 1)

            def fold_l1(_):
                pe.wait_ge(ln[1], LN_SUMS)
                pe.wait_ge(fold_v, 8)
                for t in range(DT):
                    for e in range(DT):
                        op = nc.tensor.transpose(Mb[0][:, t * D + e * P:t * D + (e + 1) * P],
                                                 shr[:, e, t * P:(t + 1) * P], ident[:])
                op.then_inc(l1_ps, 1)
                for t in range(DT):
                    nc.tensor.transpose(Mb[1][:, t * P:(t + 1) * P], kvr[:, t * P:(t + 1) * P], ident[:])
                for t in range(DT):
                    op = nc.tensor.transpose(Mb[1][:, D + t * P:D + (t + 1) * P], wor[:, t, :], ident[:])
                op.then_inc(l1_ps, 1)

            def x1T(b):
                turn(x1, "x1T", ln[1], b, LN_DONE)

            def up(b, k):
                if k == 0:
                    pe.wait_ge(dn_lo, 4)
                    pe.wait_ge(t_lo["x1T"], b * DT + DT)
                for t in range(DT):
                    op = three(Ub[k % 2][:], up_hl, x1T_hl, (slice(None), t, slice(k * P, (k + 1) * P)),
                               (slice(None), t, slice(None)), t == 0, t == DT - 1)
                op.then_inc(hid_ps, 1)

            def down_of(k, hl, first, last):
                for c in range(TT):
                    op = three(tok(Db, c), (r_hi[k % 2], r_lo[k % 2]), hl, (slice(None), slice(c * P, (c + 1) * P)),
                               (slice(None), k if hl is not sw2_hl else k - E, slice(None)), first and c % 2 == 0, last)
                    if last and c % 2:
                        op.then_inc(moe_ps if hl is not dn_hl else ffn_ps, 1)

            def down(b, k):
                pe.wait_ge(hid_lo, b * HT + k + 1)
                down_of(k, dn_hl, k == 0, k == HT - 1)

            def x2T(b):
                turn(x2, "x2T", ln[2], b, LN_DONE)

            def shift(b):
                pe.wait_ge(l1_lo, 3)
                pe.wait_ge(t_lo["x2T"], b * DT + DT)
                for c in range(TT):
                    s = (c + TT // 2) % TT
                    for t in range(DT):
                        op = three(tok(Mb, c), x2T_hl, sh_hl, (slice(None), t, slice(s * P, (s + 1) * P)),
                                   (slice(None), t, slice(None)), t == 0, t == DT - 1)
                    if c % 2:
                        op.then_inc(shift_ps, 1)

            def zT(b):
                turn(z, "zT", ln[3], b, LN_DONE)

            def kv(b):
                pe.wait_ge(t_lo["zT"], b * DT + DT)
                for t in range(DT):
                    op = three(Mb[0][:], kv_hl, zT_hl, (slice(None), t, slice(None)), (slice(None), t, slice(None)),
                               t == 0, t == DT - 1)
                op.then_inc(kv_ps, 1)

            def outp(b):
                pe.wait_ge(kv_v, b * N_KV + 3)
                for c in range(TT):
                    for n in range(2):
                        op = mm(tok(Mb, c), st_hl[:, c * P:(c + 1) * P], wo_hl[n][:], start=n == 0, stop=n == 1,
                                skip_group_check=True)
                    if c % 2:
                        op.then_inc(out_ps, 1)

            def x3T(b):
                turn(x3[slot(b)], "x3T", ln[4], b, LN_DONE)

            def logits(b):
                pe.wait_ge(wsplit, 12)
                pe.wait_ge(t_lo["x3T"], b * DT + DT)
                for c in range(TT):
                    for t in range(DT):
                        op = three(Mb[1][:, c * E:(c + 1) * E], x3T_hl[slot(b)], gw_hl,
                                   (slice(None), t, slice(c * P, (c + 1) * P)), (slice(None), t, slice(None)),
                                   t == 0, t == DT - 1)
                op.then_inc(logit_ps, 1)

            def gT(b):
                pe.wait_ge(gate_v, b * N_GATE + N_GATE)
                for n, src in enumerate((gA, gB)):
                    for c in range(TT):
                        op = nc.tensor.transpose(Tb[n][:, c * P:(c + 1) * P], src[:, c, :], ident[:])
                    op.then_inc(gT_ps, 1)

            def eup(b, k):
                if k == 0:
                    pe.wait_ge(wsplit, 12)
                w, cols = (w1_hl, (slice(None), k)) if k < E else (sw1_hl, (slice(None),))
                for t in range(DT):
                    at = (*cols, t, slice(None)) if k < E else (slice(None), t, slice((k - E) * P, (k - E + 1) * P))
                    op = three(Ub[k % 2][:], w, x3T_hl[slot(b)], at, (slice(None), t, slice(None)), t == 0, t == DT - 1)
                op.then_inc(mhid_ps, 1)

            def gbias(b):
                pe.wait_ge(gT_sb, b * 3 + 3)
                pe.wait_ge(ln[2], (b + 1) * LN_DONE + LN_SUMS) if not (isinstance(b, int) and b == B - 1) else \
                    pe.wait_ge(ln[5], (b - 1) * LN_DONE + LN_SUMS)
                for c in range(TT):
                    for n in range(2):
                        mm(tok(Db, c), gAT_r[:, c * P:(c + 1) * P], b2_hl[n][:], start=n == 0 and c % 2 == 0, stop=False,
                           skip_group_check=True)

            def edown(b, k):
                pe.wait_ge(mhid_lo, b * NU + k + 1)
                down_of(k, w2_hl if k < E else sw2_hl, False, k == NU - 1)

            run(pe, {"xT": xT, "energy": energy, "PT": PT, "attn": attn, "fold_up": fold_up, "fold_down": fold_down,
                     "fold_l1": fold_l1, "x1T": x1T, "up": up, "down": down, "x2T": x2T, "shift": shift, "zT": zT,
                     "kv": kv, "outp": outp, "x3T": x3T, "logits": logits, "gT": gT, "eup": eup, "gbias": gbias,
                     "edown": edown})


_INS = ["L0_attn_x", "L0_ffn_w_up_q", "L0_ffn_w_up_scale", "L0_ffn_b_up", "L0_ffn_w_up_lora_a",
        "L0_ffn_w_up_lora_b", "L0_ffn_w_down_q", "L0_ffn_w_down_scale", "L0_ffn_b_down",
        "L0_ffn_w_down_lora_a", "L0_ffn_w_down_lora_b", "L1_attn_W_key", "L1_attn_W_value",
        "L1_attn_W_output", "L1_attn_W_shift", "L1_attn_gate", "L1_attn_time_decay",
        "L1_attn_time_first", "L1_attn_ln_gamma", "L1_attn_ln_beta", "L1_ffn_gate_w", "L1_ffn_w1",
        "L1_ffn_b1", "L1_ffn_w2", "L1_ffn_b2", "L1_ffn_shared_w1", "L1_ffn_shared_b1",
        "L1_ffn_shared_w2", "L1_ffn_shared_b2"]


def kernel(**inputs):
    import numpy as np
    import concourse.bacc as bacc
    from concourse.bass_utils import run_bass_kernel_spmd

    nc = bacc.Bacc("TRN2", target_bir_lowering=False, num_devices=1)
    arrays, args = {}, []
    for name in _INS:
        a = np.ascontiguousarray(inputs[name])
        arrays[f"in_{name}"] = a
        args.append(nc.dram_tensor(f"in_{name}", a.shape, mybir.dt.from_np(a.dtype), kind="ExternalInput").ap())
    shape = inputs["L0_attn_x"].shape
    args.append(nc.dram_tensor("out_x", shape, F32, kind="ExternalOutput").ap())
    post_ln_kernel(nc, *args)
    r = run_bass_kernel_spmd(nc, [arrays], core_ids=[0])
    return r.results[0]["out_x"]
```

```python
from contextlib import ExitStack

import concourse.bass as bass
from concourse import mybir

F32 = mybir.dt.float32
F32R = mybir.dt.float32r
I32 = mybir.dt.int32
ALU = mybir.AluOpType
ACT = mybir.ActivationFunctionType
AX = mybir.AxisListType

P = 128
EPS = 1e-5
BLOCK = 64
RING = 3
FILLER = -3.0e38
TAKEN = 3.0e38

PLAN = {
    "start": [("x_split", 0), ("xT", 0), ("energy", 0), ("softmax", 0), ("fold_up", 0), ("PT", 0),
              ("fold_down", 0), ("ln_stats", 0, 1), ("attn", 0), ("ln_apply", 0, 1), ("fold_l1", 0),
              ("x1T", 0)],
    "first": [3, 3, 4, 5, 6, 8, 8, 9, 16, 5, 5, 5, 6, 8, 16],
    "second": [1, 2, 2, 2, 5, 7, 7, 9, 9, 9, 12, 13, 15, 16],
    "L0": [0, 1, 3, 3, 8, 12, 12, 13, 16],
    "L1": [17, 19, 19, 19, 23, 27, 27, 32, 32, 33, 35, 36, 37, 39],
    "last": [2, 6, 6, 8, 10, 11, 12, 14, 14, 15, 18, 18, 18, 21],
}

LN_SUMS, LN_STATS, LN_AGGR, LN_DONE = 2, 6, 10, 14


def post_ln_kernel(nc, x, up_q, up_scale, b_up, up_a, up_b, dn_q, dn_scale, b_down, dn_a, dn_b,
                   w_key, w_value, w_output, w_shift, gate, time_decay, time_first, ln_gamma,
                   ln_beta, gate_w, w1, b1, w2, b2, sw1, sb1, sw2, sb2, out):
    B, T, D = x.shape
    H = up_q.shape[0]
    R = up_a.shape[1]
    S = w_key.shape[0]
    E = gate_w.shape[1]
    DT, TT, HT = D // P, T // P, H // P
    SHT = sw1.shape[1] // P
    NU = E + SHT
    assert (D, T, S, E, w1.shape[2], B) == (256, 512, 64, 8, P, 4)

    with ExitStack() as ctx:
        def sb(name, shape, dt=F32):
            return ctx.enter_context(nc.sbuf_tensor(name, shape, dt))

        def pair(name, shape):
            return sb(name + "_hi", shape, F32R), sb(name + "_lo", shape, F32R)

        def sem(name):
            return ctx.enter_context(nc.semaphore(name))

        def f32(ap):
            return ap.bitcast(F32)

        bank = {n: ctx.enter_context(nc.psum_tensor(n, [P, 512], F32))
                for n in ("T0", "T1", "U0", "U1", "D0", "D1", "M0", "M1")}
        Tb = [bank["T0"], bank["T1"]]
        Ub = [bank["U0"], bank["U1"]]
        Db = [bank["D0"], bank["D1"]]
        Mb = [bank["M0"], bank["M1"]]

        def tok(banks, t):
            return banks[t // 2][:, (t % 2) * D:(t % 2 + 1) * D]

        ident = sb("ident", [P, P])
        up_hl = pair("up_w", [P, DT, H])
        dn_hl = pair("dn_w", [P, HT, D])
        sh_hl = pair("shift_w", [P, DT, D])
        kv_hl = pair("kv_w", [P, DT, P])
        wo_hl = pair("out_w", [P, D])
        gw_hl = pair("gate_w", [P, DT, E])
        w1_hl = pair("w1_w", [P, E, DT, P])
        w2_hl = pair("w2_w", [P, E, D])
        sw1_hl = pair("sw1_w", [P, DT, SHT * P])
        sw2_hl = pair("sw2_w", [P, SHT, D])
        b2_hl = pair("b2_rows", [P, D])
        bup_c = sb("bup_c", [P, HT])
        b1_c = sb("b1_c", [P, NU])
        bdown_bc = sb("bdown_bc", [P, D])
        decay = sb("decay", [P, T])
        kvc = sb("kvc", [P, 4])
        stage_moe = sb("stage_moe", [P, E * T])
        stage_q = sb("stage_q", [P, HT * D + DT * H])
        stage_lora = sb("stage_lora", [P, 3 * H])
        stage_sw = sb("stage_sw", [P, 2 * T])

        def view(buf, at, *shape):
            n = shape[0] * (shape[1] if len(shape) > 1 else 1) * (shape[2] if len(shape) > 2 else 1)
            ap = buf[:, at:at + n]
            if len(shape) == 2:
                return ap.rearrange("p (a b) -> p a b", a=shape[0])
            if len(shape) == 3:
                return ap.rearrange("p (a b c) -> p a b c", a=shape[0], b=shape[1])
            return ap

        w1r = view(stage_moe, 0, E, DT, P)
        w2r = view(stage_moe, E * D, E, D)
        GB = 4
        gbc = view(stage_moe, 0, GB, T)
        x3_0 = view(stage_moe, GB * T, TT, D)
        x2keep = view(stage_moe, GB * T + TT * D, TT, D)
        z = x2keep
        wq = view(stage_q, 0, HT, D)
        wqd = view(stage_q, HT * D, DT, H)
        upq, dnq = wq.bitcast(I32), wqd.bitcast(I32)
        x2 = view(stage_q, 0, TT, D)
        x1 = view(stage_q, TT * D, TT, D)
        x1res = view(stage_q, 2 * TT * D, TT, D)
        r_01 = view(stage_q, 3 * TT * D, 2, T)
        upb = view(stage_lora, 0, H)
        dna = view(stage_lora, H, HT, P)
        dnaT = view(stage_lora, 2 * H, H)
        tanh_k = view(stage_lora, 0, T)
        ex_k = view(stage_lora, T, T)
        wkv = view(stage_lora, 2 * T, T)
        states = view(stage_lora, 3 * T, T)
        rbuf = [r_01[:, 0, :], r_01[:, 1, :], view(stage_lora, 2 * H, T)]
        sw1r = view(stage_sw, 0, DT, SHT * P)
        sw2r = view(stage_sw, T, SHT, D)
        gAT = view(stage_sw, 0, T)
        gBT = view(stage_sw, T, T)
        ups = sb("ups", [P, HT, D // BLOCK])
        dns = sb("dns", [P, DT, H // BLOCK])
        obuf = sb("obuf", [P, TT, D])
        upa = obuf[:, 0, :].rearrange("p (t r) -> p t r", t=DT)
        dnb, upaT, gamma_bc = obuf[:, 1, :], obuf[:, 2, :], obuf[:, 3, :]
        gA = sb("gA", [P, TT, P])
        gB = sb("gB", [P, TT, P])
        shr = gA[:].rearrange("p t c -> p (t c)").rearrange("p (t d) -> p t d", t=DT)
        kvr = gB[:, 0:2, :].rearrange("p t c -> p (t c)")
        wor = gB[:, 2:4, :]
        gwr = sb("gwr", [P, DT, E])
        b2r = sb("b2r", [P, D])
        gate_bc = sb("gate_bc", [P, D])
        keep_bc = gate_bc
        gate_c = sb("gate_c", [P, 2 * DT])
        beta_bc = sb("beta_bc", [P, D])
        tdec = sb("tdec", [P, 2])
        mhalf = sb("mhalf", [P, TT])
        pad = sb("pad", [P, 1])
        xin = sb("xin", [P, TT, D])
        x_hl = pair("x_or_x2T", [P, TT * D])
        x2T_hl = [p[:].rearrange("p (t n) -> p t n", t=DT) for p in x_hl]
        x_hl = [p[:].rearrange("p (t n) -> p t n", t=TT) for p in x_hl]
        xT_hl = pair("xT_or_zT", [P, DT, T])
        zT_hl = xT_hl
        mx = sb("mx", [P, DT])
        nmx = sb("nmx", [P, DT])
        esum = sb("esum", [P, DT])
        erec = sb("erec", [P, DT])
        prob = sb("prob", [P, DT, D])
        kvb = prob[:, 0, :]
        PT_hl = pair("PT", [P, DT, D])
        x1T_hl = pair("x1T", [P, DT, T])
        st_hl = PT_hl[0][:].rearrange("p t d -> p (t d)")
        x3 = [x3_0, x1]
        x3T_hl = [pair("x3T", [P, DT, T]), x1T_hl]
        logit = sb("logit", [P, TT, 2 * E])
        top = sb("top", [P, TT, 8])
        marked = sb("marked", [P, TT, 2 * E])
        chosen = sb("chosen", [P, TT, E])
        gexp = sb("gexp", [P, TT, E])
        gsum = sb("gsum", [P, TT])
        gates = sb("gates", [P, TT, E])
        gates_hi = sb("gates_hi", [P, TT, E], F32R)
        gAT_r = sb("gAT_r", [P, T], F32R)
        r_hi = [sb(f"r_hi{i}", [P, T], F32R) for i in range(RING)]
        r_lo = [sb(f"r_lo{i}", [P, T], F32R) for i in range(RING)]
        stats = sb("stats", [P, TT, 6])
        mv = {n: sb(f"mv{n}", [P, TT, 2]) for n in range(1, 6)}
        veps = sb("veps", [P, TT])
        rstd = {n: sb(f"rstd{n}", [P, TT]) for n in range(1, 6)}

        ld_x = sem("ld_x")
        ld_up = sem("ld_up")
        ld_dn = sem("ld_dn")
        ld_l1 = sem("ld_l1")
        ld_bc = sem("ld_bc")
        ld_moe = sem("ld_moe")
        saved = sem("saved")
        zeroed = sem("zeroed")
        id_ready = sem("id_ready")
        const_ready = sem("const_ready")
        fold_v = sem("fold_v")
        fold_a = sem("fold_a")
        lora_t = sem("lora_t")
        lora_sb = sem("lora_sb")
        up_ps = sem("up_ps")
        up_hi = sem("up_hi")
        up_lo = sem("up_lo")
        dn_ps = sem("dn_ps")
        dn_hi = sem("dn_hi")
        dn_lo = sem("dn_lo")
        l1_ps = sem("l1_ps")
        l1_hi = sem("l1_hi")
        l1_lo = sem("l1_lo")
        wsplit = sem("wsplit")
        t_ps = {n: sem(f"ps_{n}") for n in ("xT", "x1T", "x2T", "zT", "x3T")}
        t_hi = {n: sem(f"hi_{n}") for n in t_ps}
        t_lo = {n: sem(f"lo_{n}") for n in t_ps}
        ln = {n: sem(f"ln{n}") for n in range(1, 6)}
        ln_eps = {n: sem(f"ln_eps{n}") for n in range(1, 6)}
        ln_r = {n: sem(f"ln_rstd{n}") for n in range(1, 6)}
        x_hi = sem("x_hi")
        x_parts = sem("x_parts")
        energy_ps = sem("energy_ps")
        soft_v = sem("soft_v")
        soft_e = sem("soft_e")
        PT_ps = sem("PT_ps")
        PT_hi = sem("PT_hi")
        PT_lo = sem("PT_lo")
        attn_ps = sem("attn_ps")
        res1 = sem("res1")
        hid_ps = sem("hid_ps")
        hid_r = sem("hid_r")
        hid_hi = sem("hid_hi")
        hid_lo = sem("hid_lo")
        ffn_ps = sem("ffn_ps")
        keep2 = sem("keep2")
        shift_ps = sem("shift_ps")
        kv_ps = sem("kv_ps")
        kv_act = sem("kv_act")
        kv_v = sem("kv_v")
        st_hi = sem("st_hi")
        out_ps = sem("out_ps")
        logit_ps = sem("logit_ps")
        gate_v = sem("gate_v")
        gate_e = sem("gate_e")
        gT_ps = sem("gT_ps")
        gT_sb = sem("gT_sb")
        g_bc = sem("g_bc")
        mhid_ps = sem("mhid_ps")
        mhid_r = sem("mhid_r")
        mhid_g = sem("mhid_g")
        mhid_hi = sem("mhid_hi")
        mhid_lo = sem("mhid_lo")
        moe_ps = sem("moe_ps")

        LN_OF = {1: (attn_ps, Mb), 2: (ffn_ps, Db), 3: (shift_ps, Mb), 4: (out_ps, Mb),
                 5: (moe_ps, Db)}
        N_SPLIT = 2 * (4 + E)
        N_GATE, N_SOFT, N_KV = 21, 5, 3

        FOLD_MOE = [("fold_moe", n, 6) for n in range(6)]
        L0 = [("x_split",), ("xT",), ("energy",), ("softmax",), ("PT",), ("attn",),
              ("ln_stats", 1), ("ln_apply", 1), ("x1T",)]
        L1 = [("x2T",), ("shift",), ("ln_stats", 3), ("ln_apply", 3), ("zT",), ("kv",), ("wkv",),
              ("outp",), ("ln_stats", 4), ("ln_apply", 4), ("x3T",), ("logits",), ("gating",),
              ("gT",)]
        def units(b, up, down, n, before=(), after=()):
            res = [(up, b, k) for k in range(LAG)] + list(before)
            for k in range(n):
                res += ([(up, b, k + LAG)] if k + LAG < n else []) + [(down, b, k)]
            return res

        LAG = 2

        def dense(m, f):
            res = []
            if m is not None:
                res = units(m, "eup", "edown", NU, before=[("gbias", m)])
            if f is not None:
                rest = units(f, "up", "down", HT)
                if m is not None:
                    res[-2:] = [rest[0], res[-2], rest[1], res[-1]]
                    rest = rest[LAG:]
            if m is not None:
                res += [("ln_stats", m, 5), ("ln_apply", m, 5)]
            if f is not None:
                res += rest + [("ln_stats", f, 2), ("ln_apply", f, 2)]
            return res

        def of(b, steps):
            return [(s[0], b, *s[1:]) for s in steps]

        def woven(main, side, at):
            res = []
            for i, s in enumerate(main):
                res.append(s)
                res += [side[n] for n, a in enumerate(at) if a == i]
            return res

        PROLOGUE = (PLAN["start"] + woven(dense(None, 0), of(1, L0) + FOLD_MOE[:6], PLAN["first"])
                    + woven(dense(None, 1), of(0, L1), PLAN["second"]))

        def middle(i):
            return woven(dense(i - 1, i + 1), of(i + 1, L0) + of(i, L1), PLAN["L0"] + PLAN["L1"])

        LAST = woven(dense(B - 2, None), of(B - 1, L1), PLAN["last"]) + dense(B - 1, None)

        def slot(b):
            return 1 if isinstance(b, int) and b == B - 1 else 0

        def run(eng, ops):
            for s in PROLOGUE:
                if s[0] in ops:
                    ops[s[0]](*s[1:])
            for i in range(1, B - 1):
                for s in middle(i):
                    if s[0] in ops:
                        ops[s[0]](*s[1:])
            for s in LAST:
                if s[0] in ops:
                    ops[s[0]](*s[1:])

        block = ctx.enter_context(nc.Block())

        @block.sync
        def _(sp):
            def load_x(b):
                sp.dma_start(xin[:], x[b].rearrange("(t p) d -> p t d", p=P)).then_inc(ld_x, 16)

            load_x(0)
            sp.dma_start(upq, up_q.rearrange("(k p) d -> p k d", p=P)).then_inc(ld_up, 16)
            sp.dma_start(ups[:], up_scale.rearrange("(k p) c -> p k c", p=P)).then_inc(ld_up, 16)
            sp.wait_ge(zeroed, 1)
            sp.dma_start(upa[:, :, 0:R], up_a.rearrange("(t p) r -> p t r", p=P)).then_inc(ld_up, 16)
            sp.dma_start(upb[0:R, :], up_b).then_inc(ld_up, 16)
            sp.dma_start(bup_c[:], b_up.rearrange("(k p) -> p k", p=P),
                         allow_slow_non_contiguous=True).then_inc(ld_up, 16)
            sp.dma_start(dnq, dn_q.rearrange("(t p) h -> p t h", p=P)).then_inc(ld_dn, 16)
            sp.dma_start(dns[:], dn_scale.rearrange("(t p) c -> p t c", p=P)).then_inc(ld_dn, 16)
            sp.dma_start(dna[:, :, 0:R], dn_a.rearrange("(k p) r -> p k r", p=P)).then_inc(ld_dn, 16)
            sp.dma_start(dnb[0:R, :], dn_b).then_inc(ld_dn, 16)
            sp.dma_start(w1r, w1.rearrange("e (t p) h -> p e t h", p=P)).then_inc(ld_moe, 16)
            sp.dma_start(w2r, w2.rearrange("e p d -> p e d")).then_inc(ld_moe, 16)
            sp.dma_start(sw1r, sw1.rearrange("(t p) h -> p t h", p=P)).then_inc(ld_moe, 16)
            sp.dma_start(sw2r, sw2.rearrange("(t p) d -> p t d", p=P)).then_inc(ld_moe, 16)
            sp.dma_start(b2r[1:1 + E, :], b2).then_inc(ld_moe, 16)
            sp.dma_start(b2r[1 + E:1 + 2 * E, :], b2).then_inc(ld_moe, 16)
            sp.dma_start(b2r[1 + 2 * E:2 + 2 * E, :], sb2.rearrange("(a d) -> a d", a=1)).then_inc(ld_moe, 16)
            sp.dma_start(b1_c[:, 0:E], b1.rearrange("e p -> p e"),
                         allow_slow_non_contiguous=True).then_inc(ld_moe, 16)
            sp.dma_start(b1_c[:, E:NU], sb1.rearrange("(k p) -> p k", p=P),
                         allow_slow_non_contiguous=True).then_inc(ld_moe, 16)
            sp.dma_start(gwr[:], gate_w.rearrange("(t p) e -> p t e", p=P)).then_inc(ld_moe, 16)

            sp.wait_ge(ln[1], LN_SUMS)
            load_x(1)

            def save(b):
                sp.wait_ge(ln[5], b * LN_DONE + LN_DONE)
                sp.dma_start(out[b].rearrange("(t p) d -> p t d", p=P), obuf[:]).then_inc(saved, 16)

            for i in range(1, B - 1):
                sp.wait_ge(ln[1], i * LN_DONE + LN_SUMS)
                sp.dma_start(xin[:], x.rearrange("b (t p) d -> b p t d", p=P)[bass.ds(i + 1, 1)].rearrange("a p t d -> (a p) t d")).then_inc(ld_x, 16)
                sp.wait_ge(ln[5], (i - 1) * LN_DONE + LN_DONE)
                sp.dma_start(out.rearrange("b (t p) d -> b p t d", p=P)[bass.ds(i - 1, 1)].rearrange("a p t d -> (a p) t d"), obuf[:]).then_inc(saved, 16)
            for b in (B - 2, B - 1):
                save(b)
            sp.wait_ge(saved, 16 * (B + 1))

        @block.gpsimd
        def _(pool):
            g = nc.gpsimd
            g.memset(ident[:], 0.0).then_inc(id_ready, 1)
            pool.wait_ge(id_ready, 1)
            g.affine_select(out=ident[:], in_=ident[:], compare_op=ALU.not_equal, fill=1.0, base=0,
                            pattern=[[-1, P]], channel_multiplier=1).then_inc(id_ready, 1)
            for zero in (upa, upb, dna, dnb, b2r[:]):
                op = g.memset(zero, 0.0)
            op.then_inc(zeroed, 1)
            g.memset(mhalf[:], -0.5).then_inc(const_ready, 1)
            g.memset(logit[:], FILLER).then_inc(const_ready, 1)

            def ln_stats(b, n):
                if n == 1:
                    pool.wait_ge(const_ready, 3)
                pool.wait_ge(ln[n], b * LN_DONE + LN_AGGR)
                g.tensor_scalar(veps[:], mv[n][:, :, 1], EPS, None, ALU.add).then_inc(ln_eps[n], 1)
                pool.wait_ge(ln_eps[n], b + 1)
                g.tensor_tensor(rstd[n][:], veps[:], mhalf[:], ALU.pow).then_inc(ln_r[n], 1)

            def bias_row(b):
                pool.wait_ge(ld_bc, 16 * 5)
                if isinstance(b, int) and b == 0:
                    pool.wait_ge(dn_lo, 4)
                else:
                    pool.wait_ge(ln[2], (b - 1) * LN_DONE + LN_SUMS)
                pool.wait_ge(ln[1], b * LN_DONE + LN_DONE)
                for t in range(TT):
                    op = g.tensor_tensor(x1res[:, t, :], x1[:, t, :], bdown_bc[:], ALU.add)
                    op.then_inc(res1, 1)

            def keep_row(b):
                pool.wait_ge(fold_a, 3)
                pool.wait_ge(fold_v, 8)
                pool.wait_ge(wsplit, N_SPLIT)
                pool.wait_ge(ln[2], b * LN_DONE + LN_DONE)
                for t in range(TT):
                    g.tensor_tensor(x2keep[:, t, :], x2[:, t, :], keep_bc[:], ALU.mult).then_inc(keep2, 1)

            small = [(gw_hl, gwr, slice(None)), (b2_hl, b2r, slice(None)), (sw1_hl, sw1r, slice(None)),
                     (sw2_hl, sw2r, slice(None))]
            parts = small + [(hl, raw, slice(e, e + 2)) for e in range(0, E, 2) for hl, raw in
                             ((w1_hl, w1r), (w2_hl, w2r))]

            def fold_moe(piece, pieces):
                pool.wait_ge(ld_moe, 16 * 10)
                for n in range(len(parts) * piece // pieces, len(parts) * (piece + 1) // pieces):
                    hl, raw, e = parts[n]
                    if raw is gwr or raw is b2r:
                        raw = raw[:]
                    if n < len(small):
                        hi, lo = hl[0][:], hl[1][:]
                    else:
                        hi, lo, raw = hl[0][:, e], hl[1][:, e], raw[:, e]
                    g.tensor_copy(hi, raw).then_inc(wsplit, 1)
                    pool.wait_ge(wsplit, 2 * n + 1)
                    g.tensor_tensor(lo, raw, f32(hi), ALU.subtract).then_inc(wsplit, 1)

            def fold_l1(_):
                pool.wait_ge(l1_ps, 2)
                g.memset(gA[:], 0.0).then_inc(const_ready, 1)
                pool.wait_ge(const_ready, 4)
                g.memset(gA[:, :, 1 + 2 * E:2 + 2 * E], 1.0).then_inc(const_ready, 1)
                g.memset(gB[:], 0.0).then_inc(const_ready, 1)

            def gT(b):
                pool.wait_ge(gT_sb, b * 3 + 1)
                for e in range(GB):
                    g.drain()
                    g.partition_broadcast(gbc[:, e, :], gAT[32 * e:32 * e + 1, :],
                                          channels=P).then_inc(g_bc, 1)
                g.drain()

            def eup(b, k):
                if k + GB < E:
                    pool.wait_ge(gT_sb, b * 3 + 2)
                    pool.wait_ge(mhid_g, b * E + k + 1)
                    g.drain()
                    g.partition_broadcast(gbc[:, k, :], gBT[32 * k:32 * k + 1, :],
                                          channels=P).then_inc(g_bc, 1)
                    g.drain()

            def ln_apply(b, n):
                if n == 1:
                    bias_row(b)
                if n == 2:
                    keep_row(b)

            run(pool, {"ln_stats": ln_stats, "ln_apply": ln_apply, "gT": gT,
                       "eup": eup, "fold_moe": fold_moe, "fold_l1": fold_l1})

        @block.scalar
        def _(act):
            a = nc.scalar
            for dst, src in ((bdown_bc, b_down), (gate_bc, gate), (gamma_bc, ln_gamma),
                             (beta_bc, ln_beta)):
                act.dma_start(dst[:], src.rearrange("(a d) -> a d", a=1).to_broadcast((P, D))).then_inc(ld_bc, 16)
            act.dma_start(gate_c[:, 0:DT], gate.rearrange("(t p) -> p t", p=P),
                          allow_slow_non_contiguous=True).then_inc(ld_bc, 16)
            act.dma_start(shr[:], w_shift.rearrange("(t p) d -> p t d", p=P)).then_inc(ld_l1, 16)
            act.dma_start(kvr[0:S, :], w_value).then_inc(ld_l1, 16)
            act.dma_start(kvr[S:2 * S, :], w_key).then_inc(ld_l1, 16)
            act.dma_start(wor[:, :, 0:S], w_output.rearrange("(t p) s -> p t s", p=P)).then_inc(ld_l1, 16)
            act.dma_start(wor[:, :, S:2 * S], w_output.rearrange("(t p) s -> p t s", p=P)).then_inc(ld_l1, 16)
            act.dma_start(tdec[0:S, 0:1], time_decay.rearrange("(s a) -> s a", a=1)).then_inc(ld_l1, 16)
            act.dma_start(tdec[S:2 * S, 0:1], time_first.rearrange("(s a) -> s a", a=1)).then_inc(ld_l1, 16)

            def x_split(b):
                act.wait_ge(ld_x, b * 16 + 16)
                if not (isinstance(b, int) and b < 2):
                    act.wait_ge(shift_ps, (b - 2) * 2 + 2)
                for i in range(2):
                    half = slice(2 * i, 2 * i + 2)
                    a.activation(x_hl[0][:, half, :], xin[:, half, :], ACT.Copy).then_inc(x_hi, 1)

            def turned(name, hl, b):
                for t in range(DT):
                    act.wait_ge(t_ps[name], b * DT + t + 1)
                    a.activation(hl[0][:, t, :], Tb[t][:], ACT.Copy).then_inc(t_hi[name], 1)

            def softmax(b):
                act.wait_ge(soft_v, b * N_SOFT + 2)
                for i in range(DT):
                    a.activation(prob[:, i, :], Mb[0][:, i * D:(i + 1) * D], ACT.Exp, bias=nmx[:, i:i + 1],
                                 accum_out=esum[:, i:i + 1]).then_inc(soft_e, 1)

            def PT(b):
                act.wait_ge(PT_ps, b + 1)
                a.activation(PT_hl[0][:].rearrange("p t d -> p (t d)"), Mb[1][:], ACT.Copy).then_inc(PT_hi, 1)

            def fold_up(_):
                act.wait_ge(lora_t, 1)
                a.activation(upaT[:], Db[1][:, 0:D], ACT.Copy).then_inc(lora_sb, 1)
                for i in range(2):
                    act.wait_ge(lora_t, 2 + i)
                    a.activation(dnaT[:, i * 512:(i + 1) * 512], Ub[i][:], ACT.Copy).then_inc(lora_sb, 1)
                for n in range(4):
                    act.wait_ge(up_ps, n + 1)
                    a.activation(up_hl[0][:, n // 2, (n % 2) * 512:(n % 2 + 1) * 512], (Db + Ub)[n][:],
                                 ACT.Copy).then_inc(up_hi, 1)

            def fold_down(_):
                for n in range(4):
                    act.wait_ge(dn_ps, n + 1)
                    a.activation(dn_hl[0][:, 2 * n:2 * n + 2, :].rearrange("p k d -> p (k d)"),
                                 (Db + Ub)[n][:], ACT.Copy).then_inc(dn_hi, 1)
                act.wait_ge(ld_bc, 16 * 5)
                a.activation(gate_bc[:], gate_bc[:], ACT.Tanh, scale=0.5).then_inc(fold_a, 1)
                a.activation(gate_c[:, DT:2 * DT], gate_c[:, 0:DT], ACT.Tanh, scale=0.5).then_inc(fold_a, 1)
                act.wait_ge(ld_l1, 16 * 7)
                a.activation(tdec[:, 1:2], tdec[:, 0:1], ACT.Exp).then_inc(fold_a, 1)

            def fold_l1(_):
                act.wait_ge(l1_ps, 1)
                a.activation(sh_hl[0][:].rearrange("p t d -> p (t d)"), Mb[0][:], ACT.Copy).then_inc(l1_hi, 1)
                act.wait_ge(l1_ps, 2)
                a.activation(kv_hl[0][:].rearrange("p t d -> p (t d)"), Mb[1][:, 0:D], ACT.Copy).then_inc(l1_hi, 1)
                a.activation(wo_hl[0][:], Mb[1][:, D:2 * D], ACT.Copy).then_inc(l1_hi, 1)

            def up(b, k):
                act.wait_ge(hid_ps, b * HT + k + 1)
                a.activation(rbuf[(NU + k) % RING], Ub[k % 2][:], ACT.Relu, bias=bup_c[:, k:k + 1]).then_inc(hid_r, 1)
                act.wait_ge(hid_r, b * HT + k + 1)
                a.activation(r_hi[(NU + k) % RING][:], rbuf[(NU + k) % RING], ACT.Copy).then_inc(hid_hi, 1)

            def kv(b):
                act.wait_ge(kv_ps, b + 1)
                a.activation(tanh_k[S:2 * S, :], Mb[0][S:2 * S, :], ACT.Tanh, bias=kvc[S:2 * S, 1:2],
                             scale=0.5).then_inc(kv_act, 1)
                act.wait_ge(kv_act, b * 2 + 1)
                a.activation(ex_k[0:S, :], tanh_k[S:2 * S, :], ACT.Exp, bias=kvc[S:2 * S, 2:3],
                             scale=kvc[S:2 * S, 2:3]).then_inc(kv_act, 1)

            def states_hi(b):
                act.wait_ge(kv_v, b * N_KV + 2)
                a.activation(st_hl[0:S, :], states[0:S, :], ACT.Copy).then_inc(st_hi, 1)

            def gating(b):
                act.wait_ge(gate_v, b * N_GATE + 11)
                a.activation(gexp[:], gexp[:], ACT.Exp).then_inc(gate_e, 1)

            def gT(b):
                act.wait_ge(gT_ps, b * 2 + 1)
                a.activation(gAT, Tb[0][:], ACT.Copy).then_inc(gT_sb, 1)
                act.wait_ge(gT_ps, b * 2 + 2)
                a.activation(gBT, Tb[1][:], ACT.Copy).then_inc(gT_sb, 1)
                a.activation(gAT_r[:], Tb[0][:], ACT.Copy).then_inc(gT_sb, 1)

            def eup(b, k):
                r = k % RING
                act.wait_ge(mhid_ps, b * NU + k + 1)
                a.activation(rbuf[r], Ub[k % 2][:], ACT.Gelu, bias=b1_c[:, k:k + 1]).then_inc(mhid_r, 1)
                if k < E:
                    act.wait_ge(mhid_g, b * E + k + 1)
                else:
                    act.wait_ge(mhid_r, b * NU + k + 1)
                a.activation(r_hi[r][:], rbuf[r], ACT.Copy).then_inc(mhid_hi, 1)

            run(act, {
                "x_split": x_split,
                "xT": lambda b: turned("xT", xT_hl, b), "x1T": lambda b: turned("x1T", x1T_hl, b),
                "x2T": lambda b: turned("x2T", x2T_hl, b), "zT": lambda b: turned("zT", zT_hl, b),
                "x3T": lambda b: turned("x3T", x3T_hl[slot(b)], b), "softmax": softmax, "PT": PT,
                "fold_up": fold_up, "fold_down": fold_down, "fold_l1": fold_l1, "up": up, "kv": kv,
                "wkv": states_hi, "gating": gating, "gT": gT, "eup": eup})

        @block.vector
        def _(dve):
            v = nc.vector
            v.memset(pad[:], 0.0).then_inc(saved, 16)
            v.memset(decay[:], 1.0).then_inc(const_ready, 1)

            def x_split(b):
                for i in range(2):
                    half = slice(2 * i, 2 * i + 2)
                    dve.wait_ge(x_hi, b * 2 + i + 1)
                    v.tensor_tensor(x_hl[1][:, half, :], xin[:, half, :], f32(x_hl[0][:, half, :]),
                                    ALU.subtract).then_inc(x_parts, 1)

            def turned(name, hl, b):
                for t in range(DT):
                    dve.wait_ge(t_hi[name], b * DT + t + 1)
                    v.tensor_tensor(hl[1][:, t, :], Tb[t][:], f32(hl[0][:, t, :]), ALU.subtract).then_inc(t_lo[name], 1)

            def ln_stats(b, n):
                ready, banks = LN_OF[n]
                y = {1: x1, 2: x2, 3: z, 4: x3[slot(b)], 5: obuf}[n]
                res = {1: xin, 2: x1res, 3: x2keep, 4: x2, 5: x3[slot(b)]}[n]
                base = b * LN_DONE
                if n == 1 and not (isinstance(b, int) and b == 0):
                    dve.wait_ge(res1, (b - 1) * TT + TT)
                if n == 2:
                    dve.wait_ge(res1, b * TT + TT)
                if n == 3:
                    dve.wait_ge(keep2, b * TT + TT)
                if n == 5:
                    dve.wait_ge(saved, b * 16 + 16)
                for i in range(2):
                    dve.wait_ge(ready, b * 2 + i + 1)
                    v.tensor_tensor(y[:, 2 * i:2 * i + 2, :].rearrange("p t d -> p (t d)"), banks[i][:],
                                    res[:, 2 * i:2 * i + 2, :].rearrange("p t d -> p (t d)"),
                                    ALU.add).then_inc(ln[n], 1)
                for t in range(TT):
                    dve.wait_ge(ln[n], base + t // 2 + 1)
                    v.bn_stats(stats[:, t, :], y[:, t, :]).then_inc(ln[n], 1)
                for t in range(TT):
                    dve.wait_ge(ln[n], base + LN_SUMS + TT)
                    v.bn_aggr(mv[n][:, t, :], stats[:, t, :]).then_inc(ln[n], 1)

            def ln_apply(b, n):
                dst = {1: x1, 2: x2, 3: z, 4: x3[slot(b)], 5: obuf}[n]
                dve.wait_ge(ln_r[n], b + 1)
                for t in range(TT):
                    v.tensor_scalar(dst[:, t, :], dst[:, t, :], mv[n][:, t, 0:1], rstd[n][:, t:t + 1],
                                    ALU.subtract, ALU.mult).then_inc(ln[n], 1)

            def softmax(b):
                base = b * N_SOFT
                dve.wait_ge(energy_ps, b + 1)
                v.tensor_reduce(mx[:], Mb[0][:].rearrange("p (i j) -> p i j", i=DT), AX.X, ALU.max).then_inc(soft_v, 1)
                dve.wait_ge(soft_v, base + 1)
                v.tensor_scalar(nmx[:], mx[:], -1.0, None, ALU.mult).then_inc(soft_v, 1)
                dve.wait_ge(soft_e, b * DT + DT)
                v.reciprocal(erec[:], esum[:]).then_inc(soft_v, 1)
                dve.wait_ge(soft_v, base + 3)
                for i in range(DT):
                    v.tensor_scalar(prob[:, i, :], prob[:, i, :], erec[:, i:i + 1], None, ALU.mult).then_inc(soft_v, 1)

            def PT(b):
                dve.wait_ge(PT_hi, b + 1)
                v.tensor_tensor(PT_hl[1][:].rearrange("p t d -> p (t d)"), Mb[1][:],
                                f32(PT_hl[0][:]).rearrange("p t d -> p (t d)"), ALU.subtract).then_inc(PT_lo, 1)

            def dequant(dst, q, scale, n):
                v.scalar_tensor_tensor(
                    out=dst.rearrange("p k (c j) -> p (k c) j", j=BLOCK),
                    in0=q.rearrange("p k (c j) -> p (k c) j", j=BLOCK), scalar=-7.5,
                    in1=scale[:].rearrange("p k (c a) -> p (k c) a", a=1).to_broadcast((P, n, BLOCK)),
                    op0=ALU.add, op1=ALU.mult).then_inc(fold_v, 1)

            def fold_up(_):
                dve.wait_ge(ld_up, 16 * 5)
                dequant(wq, upq, ups, HT * D // BLOCK)
                for n in range(4):
                    dst = (slice(None), n // 2, slice((n % 2) * 512, (n % 2 + 1) * 512))
                    dve.wait_ge(up_hi, n + 1)
                    v.tensor_tensor(up_hl[1][dst], (Db + Ub)[n][:], f32(up_hl[0][dst]), ALU.subtract).then_inc(up_lo, 1)

            def fold_down(_):
                dve.wait_ge(ld_dn, 16 * 4)
                dequant(wqd, dnq, dns, DT * H // BLOCK)
                for n in range(4):
                    dve.wait_ge(dn_hi, n + 1)
                    v.tensor_tensor(dn_hl[1][:, 2 * n:2 * n + 2, :].rearrange("p k d -> p (k d)"), (Db + Ub)[n][:],
                                    f32(dn_hl[0][:, 2 * n:2 * n + 2, :]).rearrange("p k d -> p (k d)"),
                                    ALU.subtract).then_inc(dn_lo, 1)
                dve.wait_ge(fold_a, 2)
                v.tensor_scalar(gate_c[:, 0:DT], gate_c[:, DT:2 * DT], 0.5, 0.5, ALU.mult, ALU.add).then_inc(fold_v, 1)
                v.tensor_scalar(keep_bc[:], gate_bc[:], -0.5, 0.5, ALU.mult, ALU.add).then_inc(fold_v, 1)
                dve.wait_ge(ld_l1, 16 * 7)
                dve.wait_ge(fold_v, 4)
                for t in range(DT):
                    v.tensor_scalar(shr[:, t, :], shr[:, t, :], gate_c[:, t:t + 1], None, ALU.mult).then_inc(fold_v, 1)
                v.tensor_tensor(kvb, kvr[:], beta_bc[:], ALU.mult).then_inc(fold_v, 1)
                v.tensor_tensor(kvr[:], kvr[:], gamma_bc[:], ALU.mult).then_inc(fold_v, 1)
                dve.wait_ge(fold_v, 8)
                v.tensor_reduce(kvc[:, 0:1], kvb, AX.X, ALU.add).then_inc(fold_v, 1)
                dve.wait_ge(fold_v, 9)
                v.tensor_scalar(kvc[:, 1:2], kvc[:, 0:1], 0.5, None, ALU.mult).then_inc(fold_v, 1)
                dve.wait_ge(fold_a, 3)
                v.tensor_scalar(kvc[:, 2:3], tdec[:, 1:2], -0.5, None, ALU.mult).then_inc(fold_v, 1)
                dve.wait_ge(const_ready, 3)
                v.tensor_scalar(decay[0:S, :], decay[0:S, :], tdec[0:S, 1:2], None, ALU.mult).then_inc(fold_v, 1)

            def fold_l1(_):
                dve.wait_ge(l1_hi, 1)
                v.tensor_tensor(sh_hl[1][:].rearrange("p t d -> p (t d)"), Mb[0][:],
                                f32(sh_hl[0][:]).rearrange("p t d -> p (t d)"), ALU.subtract).then_inc(l1_lo, 1)
                dve.wait_ge(l1_hi, 3)
                v.tensor_tensor(kv_hl[1][:].rearrange("p t d -> p (t d)"), Mb[1][:, 0:D],
                                f32(kv_hl[0][:]).rearrange("p t d -> p (t d)"), ALU.subtract).then_inc(l1_lo, 1)
                v.tensor_tensor(wo_hl[1][:], Mb[1][:, D:2 * D], f32(wo_hl[0][:]), ALU.subtract).then_inc(l1_lo, 1)

            def up(b, k):
                dve.wait_ge(hid_hi, b * HT + k + 1)
                r = (NU + k) % RING
                v.tensor_tensor(r_lo[r][:], rbuf[r], f32(r_hi[r][:]), ALU.subtract).then_inc(hid_lo, 1)

            def recur(b):
                dve.wait_ge(kv_act, b * 2 + 2)
                dve.wait_ge(fold_v, 12)
                v.scalar_tensor_tensor(out=wkv[0:S, :], in0=Mb[0][0:S, :], scalar=kvc[0:S, 0:1],
                                       in1=ex_k[0:S, :], op0=ALU.add, op1=ALU.mult).then_inc(kv_v, 1)
                dve.wait_ge(kv_v, b * N_KV + 1)
                v.tensor_tensor_scan(states[0:S, :], decay[0:S, :], wkv[0:S, :], 0.0, ALU.mult, ALU.add).then_inc(kv_v, 1)
                dve.wait_ge(st_hi, b + 1)
                v.tensor_tensor(st_hl[S:2 * S, :], states[0:S, :], f32(st_hl[0:S, :]), ALU.subtract).then_inc(kv_v, 1)

            def gating(b):
                base, n = b * N_GATE, [0]

                def step(op):
                    op.then_inc(gate_v, 1)
                    n[0] += 1

                def settle():
                    dve.wait_ge(gate_v, base + n[0])

                dve.wait_ge(logit_ps, b + 1)
                dve.wait_ge(const_ready, 6)
                step(v.tensor_copy(logit[:, :, 0:E], Mb[1][:, 0:TT * E].rearrange("p (t e) -> p t e", t=TT)))
                settle()
                for t in range(TT):
                    step(v.max(top[:, t, :], logit[:, t, :]))
                settle()
                step(v.tensor_tensor(gexp[:], logit[:, :, 0:E], top[:, :, 0:1].to_broadcast((P, TT, E)), ALU.subtract))
                step(v.memset(top[:, :, 2:8], FILLER))
                settle()
                for t in range(TT):
                    step(v.match_replace(marked[:, t, :], top[:, t, :], logit[:, t, :], TAKEN))
                settle()
                step(v.tensor_scalar(chosen[:], marked[:, :, 0:E], TAKEN, None, ALU.is_equal))
                dve.wait_ge(gate_e, b + 1)
                settle()
                step(v.tensor_tensor(gates[:], gexp[:], chosen[:], ALU.mult))
                settle()
                step(v.tensor_reduce(gsum[:], gates[:], AX.X, ALU.add))
                settle()
                step(v.reciprocal(gsum[:], gsum[:]))
                settle()
                step(v.tensor_tensor(gates[:], gates[:], gsum[:].rearrange("p (t a) -> p t a", a=1).to_broadcast((P, TT, E)), ALU.mult))
                settle()
                step(v.tensor_copy(gates_hi[:], gates[:]))
                step(v.tensor_copy(gA[:].rearrange("p t (j c) -> p t j c", c=32)[:, :, :, 0], gates[:, :, 0:4]))
                step(v.tensor_copy(gB[:].rearrange("p t (j c) -> p t j c", c=32)[:, :, :, 0], gates[:, :, 4:8]))
                settle()
                step(v.tensor_copy(gA[:, :, 1:1 + E], f32(gates_hi[:])))
                step(v.tensor_tensor(gA[:, :, 1 + E:1 + 2 * E], gates[:], f32(gates_hi[:]), ALU.subtract))
                while n[0] < N_GATE:
                    step(v.memset(pad[:], 0.0))

            def eup(b, k):
                r = k % RING
                if k < E:
                    dve.wait_ge(mhid_r, b * NU + k + 1)
                    dve.wait_ge(g_bc, b * E + k + 1)
                    v.tensor_tensor(rbuf[r], rbuf[r], gbc[:, k % GB, :], ALU.mult).then_inc(mhid_g, 1)
                dve.wait_ge(mhid_hi, b * NU + k + 1)
                v.tensor_tensor(r_lo[r][:], rbuf[r], f32(r_hi[r][:]), ALU.subtract).then_inc(mhid_lo, 1)

            run(dve, {
                "x_split": x_split,
                "xT": lambda b: turned("xT", xT_hl, b), "x1T": lambda b: turned("x1T", x1T_hl, b),
                "x2T": lambda b: turned("x2T", x2T_hl, b), "zT": lambda b: turned("zT", zT_hl, b),
                "x3T": lambda b: turned("x3T", x3T_hl[slot(b)], b), "softmax": softmax, "PT": PT,
                "ln_stats": ln_stats, "ln_apply": ln_apply, "fold_up": fold_up, "fold_down": fold_down,
                "fold_l1": fold_l1, "up": up, "wkv": recur, "gating": gating, "eup": eup})

        @block.tensor
        def _(pe):
            mm = nc.tensor.matmul

            def three(dst, w_hl, m_hl, cols, rows, first, last):
                for i, (w, m) in enumerate(((0, 0), (0, 1), (1, 0))):
                    op = mm(dst, w_hl[w][cols], m_hl[m][rows], start=first and i == 0,
                            stop=last and i == 2, skip_group_check=True)
                return op

            def turn(src, name, after, b, count):
                for t in range(DT):
                    for c in range(TT):
                        if t == 0:
                            pe.wait_ge(after, b * count + count - TT + c + 1)
                        op = nc.tensor.transpose(Tb[t][:, c * P:(c + 1) * P], src[:, c, t * P:(t + 1) * P], ident[:])
                    op.then_inc(t_ps[name], 1)

            def xT(b):
                pe.wait_ge(id_ready, 2)
                pe.wait_ge(ld_x, b * 16 + 16)
                if not (isinstance(b, int) and b < 2):
                    pe.wait_ge(gT_sb, (b - 2) * 3 + 3)
                for t in range(DT):
                    for c in range(TT):
                        op = nc.tensor.transpose(Tb[t][:, c * P:(c + 1) * P], xin[:, c, t * P:(t + 1) * P], ident[:])
                    op.then_inc(t_ps["xT"], 1)

            def energy(b):
                for i in range(DT):
                    for c in range(TT):
                        if i == 0 and c % 2 == 0:
                            pe.wait_ge(x_parts, b * 2 + c // 2 + 1)
                        op = three(Mb[0][:, i * D:(i + 1) * D], x_hl, x_hl, (slice(None), c, slice(i * P, (i + 1) * P)),
                                   (slice(None), c, slice(None)), c == 0, c == TT - 1)
                op.then_inc(energy_ps, 1)

            def PT(b):
                pe.wait_ge(soft_v, b * N_SOFT + 5)
                for j in range(DT):
                    for i in range(DT):
                        op = nc.tensor.transpose(Mb[1][:, j * D + i * P:j * D + (i + 1) * P],
                                                 prob[:, i, j * P:(j + 1) * P], ident[:])
                op.then_inc(PT_ps, 1)

            def attn(b):
                pe.wait_ge(PT_lo, b + 1)
                pe.wait_ge(t_lo["xT"], b * DT + DT)
                for c in range(TT):
                    for j in range(DT):
                        op = three(tok(Mb, c), xT_hl, PT_hl, (slice(None), j, slice(c * P, (c + 1) * P)),
                                   (slice(None), j, slice(None)), j == 0, j == DT - 1)
                    if c % 2:
                        op.then_inc(attn_ps, 1)

            def fold_up(_):
                pe.wait_ge(ld_up, 16 * 5)
                for t in range(DT):
                    op = nc.tensor.transpose(Db[1][:, t * P:(t + 1) * P], upa[:, t, :], ident[:])
                op.then_inc(lora_t, 1)
                pe.wait_ge(ld_dn, 16 * 4)
                for k in range(HT):
                    op = nc.tensor.transpose(Ub[k // 4][:, k % 4 * P:(k % 4 + 1) * P], dna[:, k, :], ident[:])
                    if k % 4 == 3:
                        op.then_inc(lora_t, 1)
                pe.wait_ge(lora_sb, 3)
                pe.wait_ge(fold_v, 1)
                for n in range(4):
                    t, half = n // 2, n % 2
                    dst = (Db + Ub)[n]
                    mm(dst[:], upaT[:, t * P:(t + 1) * P], upb[:, half * 512:(half + 1) * 512], start=True,
                       stop=False, skip_group_check=True)
                    for k in range(4):
                        op = mm(dst[:, k * P:(k + 1) * P], wq[:, half * 4 + k, t * P:(t + 1) * P], ident[:],
                                start=False, stop=True, skip_group_check=True)
                    op.then_inc(up_ps, 1)

            def fold_down(_):
                pe.wait_ge(fold_v, 2)
                for n in range(4):
                    pe.wait_ge(up_lo, n + 1)
                    dst = (Db + Ub)[n]
                    for k in range(2):
                        cols = slice(k * D, (k + 1) * D)
                        mm(dst[:, cols], dnaT[:, (2 * n + k) * P:(2 * n + k + 1) * P], dnb, start=k == 0,
                           stop=False, skip_group_check=True)
                    for k in range(2):
                        for t in range(DT):
                            op = mm(dst[:, k * D + t * P:k * D + (t + 1) * P], wqd[:, t, (2 * n + k) * P:(2 * n + k + 1) * P],
                                    ident[:], start=False, stop=True, skip_group_check=True)
                    op.then_inc(dn_ps, 1)

            def fold_l1(_):
                pe.wait_ge(ln[1], LN_SUMS)
                pe.wait_ge(fold_v, 8)
                for t in range(DT):
                    for e in range(DT):
                        op = nc.tensor.transpose(Mb[0][:, t * D + e * P:t * D + (e + 1) * P],
                                                 shr[:, e, t * P:(t + 1) * P], ident[:])
                op.then_inc(l1_ps, 1)
                for t in range(DT):
                    nc.tensor.transpose(Mb[1][:, t * P:(t + 1) * P], kvr[:, t * P:(t + 1) * P], ident[:])
                for t in range(DT):
                    op = nc.tensor.transpose(Mb[1][:, D + t * P:D + (t + 1) * P], wor[:, t, :], ident[:])
                op.then_inc(l1_ps, 1)

            def x1T(b):
                turn(x1, "x1T", ln[1], b, LN_DONE)

            def up(b, k):
                if k == 0:
                    pe.wait_ge(dn_lo, 4)
                    pe.wait_ge(t_lo["x1T"], b * DT + DT)
                if k >= 2:
                    pe.wait_ge(hid_r, b * HT + k - 1)
                elif not (isinstance(b, int) and b < 2):
                    pe.wait_ge(mhid_r, (b - 2) * NU + NU - 1 + k)
                for t in range(DT):
                    op = three(Ub[k % 2][:], up_hl, x1T_hl, (slice(None), t, slice(k * P, (k + 1) * P)),
                               (slice(None), t, slice(None)), t == 0, t == DT - 1)
                op.then_inc(hid_ps, 1)

            def down_of(k, r, hl, first, last):
                for c in range(TT):
                    op = three(tok(Db, c), (r_hi[r], r_lo[r]), hl, (slice(None), slice(c * P, (c + 1) * P)),
                               (slice(None), k if hl is not sw2_hl else k - E, slice(None)), first and c % 2 == 0, last)
                    if last and c % 2:
                        op.then_inc(moe_ps if hl is not dn_hl else ffn_ps, 1)

            def down(b, k):
                pe.wait_ge(hid_lo, b * HT + k + 1)
                if k == 0 and not (isinstance(b, int) and b < 2):
                    pe.wait_ge(ln[5], (b - 2) * LN_DONE + LN_SUMS)
                down_of(k, (NU + k) % RING, dn_hl, k == 0, k == HT - 1)

            def x2T(b):
                if not (isinstance(b, int) and b == B - 1):
                    pe.wait_ge(t_lo["x1T"], (b + 1) * DT + DT)
                else:
                    pe.wait_ge(gT_sb, (b - 1) * 3 + 3)
                turn(x2, "x2T", ln[2], b, LN_DONE)

            def shift(b):
                pe.wait_ge(l1_lo, 3)
                pe.wait_ge(t_lo["x2T"], b * DT + DT)
                for c in range(TT):
                    s = (c + TT // 2) % TT
                    for t in range(DT):
                        op = three(tok(Mb, c), x2T_hl, sh_hl, (slice(None), t, slice(s * P, (s + 1) * P)),
                                   (slice(None), t, slice(None)), t == 0, t == DT - 1)
                    if c % 2:
                        op.then_inc(shift_ps, 1)

            def zT(b):
                turn(z, "zT", ln[3], b, LN_DONE)

            def kv(b):
                pe.wait_ge(t_lo["zT"], b * DT + DT)
                for t in range(DT):
                    op = three(Mb[0][:], kv_hl, zT_hl, (slice(None), t, slice(None)), (slice(None), t, slice(None)),
                               t == 0, t == DT - 1)
                op.then_inc(kv_ps, 1)

            def outp(b):
                pe.wait_ge(kv_v, b * N_KV + 3)
                for c in range(TT):
                    for n in range(2):
                        op = mm(tok(Mb, c), st_hl[:, c * P:(c + 1) * P], wo_hl[n][:], start=n == 0, stop=n == 1,
                                skip_group_check=True)
                    if c % 2:
                        op.then_inc(out_ps, 1)

            def x3T(b):
                turn(x3[slot(b)], "x3T", ln[4], b, LN_DONE)

            def logits(b):
                pe.wait_ge(wsplit, N_SPLIT)
                pe.wait_ge(t_lo["x3T"], b * DT + DT)
                for c in range(TT):
                    for t in range(DT):
                        op = three(Mb[1][:, c * E:(c + 1) * E], x3T_hl[slot(b)], gw_hl,
                                   (slice(None), t, slice(c * P, (c + 1) * P)), (slice(None), t, slice(None)),
                                   t == 0, t == DT - 1)
                op.then_inc(logit_ps, 1)

            def gT(b):
                pe.wait_ge(gate_v, b * N_GATE + N_GATE)
                for n, src in enumerate((gA, gB)):
                    for c in range(TT):
                        op = nc.tensor.transpose(Tb[n][:, c * P:(c + 1) * P], src[:, c, :], ident[:])
                    op.then_inc(gT_ps, 1)

            def eup(b, k):
                if k == 0:
                    pe.wait_ge(wsplit, N_SPLIT)
                if k >= 2:
                    pe.wait_ge(mhid_r, b * NU + k - 1)
                elif not (isinstance(b, int) and b == B - 1):
                    pe.wait_ge(hid_r, (b + 1) * HT + HT - 1 + k)
                w, cols = (w1_hl, (slice(None), k)) if k < E else (sw1_hl, (slice(None),))
                for t in range(DT):
                    at = (*cols, t, slice(None)) if k < E else (slice(None), t, slice((k - E) * P, (k - E + 1) * P))
                    op = three(Ub[k % 2][:], w, x3T_hl[slot(b)], at, (slice(None), t, slice(None)), t == 0, t == DT - 1)
                op.then_inc(mhid_ps, 1)

            def gbias(b):
                pe.wait_ge(gT_sb, b * 3 + 3)
                pe.wait_ge(ln[2], (b + 1) * LN_DONE + LN_SUMS) if not (isinstance(b, int) and b == B - 1) else \
                    pe.wait_ge(ln[5], (b - 1) * LN_DONE + LN_SUMS)
                for c in range(TT):
                    for n in range(2):
                        mm(tok(Db, c), gAT_r[:, c * P:(c + 1) * P], b2_hl[n][:], start=n == 0 and c % 2 == 0, stop=False,
                           skip_group_check=True)

            def edown(b, k):
                pe.wait_ge(mhid_lo, b * NU + k + 1)
                down_of(k, k % RING, w2_hl if k < E else sw2_hl, False, k == NU - 1)

            run(pe, {"xT": xT, "energy": energy, "PT": PT, "attn": attn, "fold_up": fold_up, "fold_down": fold_down,
                     "fold_l1": fold_l1, "x1T": x1T, "up": up, "down": down, "x2T": x2T, "shift": shift, "zT": zT,
                     "kv": kv, "outp": outp, "x3T": x3T, "logits": logits, "gT": gT, "eup": eup, "gbias": gbias,
                     "edown": edown})


_INS = ["L0_attn_x", "L0_ffn_w_up_q", "L0_ffn_w_up_scale", "L0_ffn_b_up", "L0_ffn_w_up_lora_a",
        "L0_ffn_w_up_lora_b", "L0_ffn_w_down_q", "L0_ffn_w_down_scale", "L0_ffn_b_down",
        "L0_ffn_w_down_lora_a", "L0_ffn_w_down_lora_b", "L1_attn_W_key", "L1_attn_W_value",
        "L1_attn_W_output", "L1_attn_W_shift", "L1_attn_gate", "L1_attn_time_decay",
        "L1_attn_time_first", "L1_attn_ln_gamma", "L1_attn_ln_beta", "L1_ffn_gate_w", "L1_ffn_w1",
        "L1_ffn_b1", "L1_ffn_w2", "L1_ffn_b2", "L1_ffn_shared_w1", "L1_ffn_shared_b1",
        "L1_ffn_shared_w2", "L1_ffn_shared_b2"]


def kernel(**inputs):
    import numpy as np
    import concourse.bacc as bacc
    from concourse.bass_utils import run_bass_kernel_spmd

    nc = bacc.Bacc("TRN2", target_bir_lowering=False, num_devices=1)
    arrays, args = {}, []
    for name in _INS:
        a = np.ascontiguousarray(inputs[name])
        arrays[f"in_{name}"] = a
        args.append(nc.dram_tensor(f"in_{name}", a.shape, mybir.dt.from_np(a.dtype), kind="ExternalInput").ap())
    shape = inputs["L0_attn_x"].shape
    args.append(nc.dram_tensor("out_x", shape, F32, kind="ExternalOutput").ap())
    post_ln_kernel(nc, *args)
    r = run_bass_kernel_spmd(nc, [arrays], core_ids=[0])
    return r.results[0]["out_x"]
```

```python
from contextlib import ExitStack

import concourse.bass as bass
from concourse import mybir

F32 = mybir.dt.float32
F32R = mybir.dt.float32r
I32 = mybir.dt.int32
ALU = mybir.AluOpType
ACT = mybir.ActivationFunctionType
AX = mybir.AxisListType

P = 128
EPS = 1e-5
BLOCK = 64
RING = 3
PART = 32
FILLER = -3.0e38
TAKEN = 3.0e38

PLAN = {
    "start": """
        xT.0@0 x_split.0@0 x_split.1@0 xT.1@0 deq_up@0 energy.0@0 lora_parts@0 energy.1@0 lora@0
        softmax@0 deq_down@0 soft_scale@0 fold_up.0@0 fold_up.1@0 fold_up.2@0 PT@0 fold_up.3@0
        gate_consts@0 attn.0@0 attn.1@0 ln_sum.1.0@0 ln_sum.1.1@0 ln_aggr.1@0 fold_down.0@0
        fold_down.1@0 fold_l1@0 fold_moe.0@0 fold_moe.1@0 ln_apply.1.0@0 ln_apply.1.1@0 x_split.0@1
        x_split.1@1 fold_down.2@0 fold_down.3@0 x1T.0@0 x1T.1@0 energy.0@1 energy.1@1 up.0@0 up.1@0
        up.2@0 softmax@1 down.0@0 fold_moe.2@0 soft_scale@1 down.1@0 xT.0@1 up.3@0 up.4@0 PT@1 down.2@0
        xT.1@1 up.5@0 attn.0@1 fold_moe.3@0 attn.1@1 ln_sum.1.0@1 down.3@0 ln_sum.1.1@1 ln_aggr.1@1
        up.6@0 down.4@0 fold_moe.4@0 up.7@0 down.5@0 down.6@0 ln_apply.1.0@1 down.7@0 ln_sum.2.0@0
        ln_apply.1.1@1 ln_sum.2.1@0 x1T.0@1 ln_aggr.2@0 x1T.1@1 fold_moe.5@0 ln_apply.2.0@0
        ln_apply.2.1@0 up.0@1 x2T.0@0 x2T.1@0 up.1@1 up.2@1 down.0@1 shift.0@0 shift.1@0 ln_sum.3.0@0
        ln_sum.3.1@0 ln_aggr.3@0 x_split.0@2 ln_apply.3.0@0 down.1@1 ln_apply.3.1@0 down.2@1 up.3@1
        zT.0@0 zT.1@0 down.3@1 kv@0 wkv@0 up.4@1 states@0 up.5@1 outp@0 ln_sum.4.0@0 down.4@1
        ln_sum.4.1@0 ln_aggr.4@0 x_split.1@2 ln_apply.4.0@0 ln_apply.4.1@0 up.6@1 up.7@1 down.5@1
        x3T.0@0 x3T.1@0 energy.0@2 logits@0 gating@0 down.6@1 energy.1@2 gate_exp@0 gate_rows@0 down.7@1
        softmax@2 ln_sum.2.0@1 gT@0 ln_sum.2.1@1 ln_aggr.2@1 eup.0@0 gbias@0 eup.1@0 ln_apply.2.0@1
        ln_apply.2.1@1
    """,
    "flow": """
        soft_scale@1 eup.2@-1 xT.0@1 edown.0@-1 eup.3@-1 edown.1@-1 PT@1 xT.1@1 eup.4@-1 edown.2@-1
        eup.5@-1 edown.3@-1 x2T.0@0 x2T.1@0 attn.0@1 attn.1@1 edown.4@-1 ln_sum.1.0@1 ln_sum.1.1@1
        eup.6@-1 ln_aggr.1@1 eup.7@-1 ln_apply.1.0@1 shift.0@0 shift.1@0 ln_apply.1.1@1 ln_sum.3.0@0
        ln_sum.3.1@0 edown.5@-1 eup.8@-1 ln_aggr.3@0 edown.6@-1 eup.9@-1 x1T.0@1 x1T.1@1 edown.7@-1
        edown.8@-1 ln_apply.3.0@0 ln_apply.3.1@0 edown.9@-1 ln_sum.5.0@-1 zT.0@0 zT.1@0 ln_sum.5.1@-1
        up.0@1 up.1@1 ln_aggr.5@-1 kv@0 wkv@0 up.2@1 down.0@1 states@0 ln_apply.5.0@-1 up.3@1 down.1@1
        ln_apply.5.1@-1 down.2@1 outp@0 ln_sum.4.0@0 ln_sum.4.1@0 ln_aggr.4@0 up.4@1 ln_apply.4.0@0
        ln_apply.4.1@0 down.3@1 up.5@1 up.6@1 down.4@1 x3T.0@0 x3T.1@0 x_split.0@2 up.7@1 logits@0
        down.5@1 gating@0 x_split.1@2 down.6@1 energy.0@2 gate_exp@0 energy.1@2 down.7@1 gate_rows@0
        softmax@2 gT@0 ln_sum.2.0@1 ln_sum.2.1@1 ln_aggr.2@1 eup.0@0 eup.1@0 ln_apply.2.0@1
        ln_apply.2.1@1 gbias@0
    """,
    "end": """
        eup.2@2 edown.0@2 x2T.0@3 x2T.1@3 eup.3@2 shift.0@3 shift.1@3 ln_sum.3.0@3 ln_sum.3.1@3
        ln_aggr.3@3 ln_apply.3.0@3 edown.1@2 edown.2@2 ln_apply.3.1@3 eup.4@2 zT.0@3 zT.1@3 eup.5@2 kv@3
        wkv@3 edown.3@2 eup.6@2 states@3 edown.4@2 eup.7@2 edown.5@2 outp@3 ln_sum.4.0@3 ln_sum.4.1@3
        edown.6@2 ln_aggr.4@3 eup.8@2 ln_apply.4.0@3 ln_apply.4.1@3 edown.7@2 x3T.0@3 x3T.1@3 eup.9@2
        logits@3 gating@3 edown.8@2 edown.9@2 gate_exp@3 gate_rows@3 gT@3 ln_sum.5.0@2 ln_sum.5.1@2
        eup.0@3 gbias@3 eup.1@3 eup.2@3 edown.0@3 eup.3@3 ln_aggr.5@2 edown.1@3 eup.4@3 ln_apply.5.0@2
        edown.2@3 ln_apply.5.1@2 eup.5@3 edown.3@3 edown.4@3 eup.6@3 eup.7@3 edown.5@3 eup.8@3 edown.6@3
        eup.9@3 edown.7@3 edown.8@3 edown.9@3 ln_sum.5.0@3 ln_sum.5.1@3 ln_aggr.5@3 ln_apply.5.0@3
        ln_apply.5.1@3
    """,
}

LN_SUMS, LN_STATS, LN_AGGR, LN_DONE = 4, 6, 10, 14


def post_ln_kernel(nc, x, up_q, up_scale, b_up, up_a, up_b, dn_q, dn_scale, b_down, dn_a, dn_b,
                   w_key, w_value, w_output, w_shift, gate, time_decay, time_first, ln_gamma,
                   ln_beta, gate_w, w1, b1, w2, b2, sw1, sb1, sw2, sb2, out):
    B, T, D = x.shape
    H = up_q.shape[0]
    R = up_a.shape[1]
    S = w_key.shape[0]
    E = gate_w.shape[1]
    DT, TT, HT = D // P, T // P, H // P
    SHT = sw1.shape[1] // P
    NU = E + SHT
    assert (D, T, S, E, w1.shape[2], B) == (256, 512, 64, 8, P, 4)

    with ExitStack() as ctx:
        def sb(name, shape, dt=F32):
            return ctx.enter_context(nc.sbuf_tensor(name, shape, dt))

        def pair(name, shape):
            return sb(name + "_hi", shape, F32R), sb(name + "_lo", shape, F32R)

        def sem(name):
            return ctx.enter_context(nc.semaphore(name))

        def f32(ap):
            return ap.bitcast(F32)

        bank = {n: ctx.enter_context(nc.psum_tensor(n, [P, 512], F32))
                for n in ("T0", "T1", "U0", "U1", "D0", "D1", "M0", "M1")}
        Tb = [bank["T0"], bank["T1"]]
        Ub = [bank["U0"], bank["U1"]]
        Db = [bank["D0"], bank["D1"]]
        Mb = [bank["M0"], bank["M1"]]

        def tok(banks, t):
            return banks[t // 2][:, (t % 2) * D:(t % 2 + 1) * D]

        ident = sb("ident", [P, P])
        up_hl = pair("up_w", [P, DT, H])
        dn_hl = pair("dn_w", [P, HT, D])
        sh_hl = pair("shift_w", [P, DT, D])
        kv_hl = pair("kv_w", [P, DT, P])
        wo_hl = pair("out_w", [P, D])
        gw_parts = sb("gate_w", [P, DT, 2 * E], F32R)
        gw_hl = gw_parts[:, :, 0:E], gw_parts[:, :, E:2 * E]
        w1_hl = pair("w1_w", [P, E, DT, P])
        w2_hl = pair("w2_w", [P, E, D])
        sw1_hl = pair("sw1_w", [P, DT, SHT * P])
        sw2_hl = pair("sw2_w", [P, SHT, D])
        b2_rows = sb("b2_rows", [P, D], F32R)
        bup_c = sb("bup_c", [P, HT])
        b1_c = sb("b1_c", [P, NU])
        bdown_bc = sb("bdown_bc", [P, D])
        decay = sb("decay", [P, T])
        kvc = sb("kvc", [P, 4])
        stage_moe = sb("stage_moe", [P, E * T])
        stage_q = sb("stage_q", [P, HT * D + DT * H])
        stage_lora = sb("stage_lora", [P, 3 * H])
        stage_sw = sb("stage_sw", [P, 2 * T])

        def view(buf, at, *shape):
            n = shape[0] * (shape[1] if len(shape) > 1 else 1) * (shape[2] if len(shape) > 2 else 1)
            ap = buf[:, at:at + n]
            if len(shape) == 2:
                return ap.rearrange("p (a b) -> p a b", a=shape[0])
            if len(shape) == 3:
                return ap.rearrange("p (a b c) -> p a b c", a=shape[0], b=shape[1])
            return ap

        w1r = view(stage_moe, 0, E, DT, P)
        w2r = view(stage_moe, E * D, E, D)
        GB = 4
        gbc = view(stage_moe, 0, GB, T)
        x3_0 = view(stage_moe, GB * T, TT, D)
        x2keep = view(stage_moe, GB * T + TT * D, TT, D)
        z = x2keep
        wq = view(stage_q, 0, HT, D)
        wqd = view(stage_q, HT * D, DT, H)
        upq, dnq = wq.bitcast(I32), wqd.bitcast(I32)
        x2 = view(stage_q, 0, TT, D)
        x1 = view(stage_q, TT * D, TT, D)
        x1res = view(stage_q, 2 * TT * D, TT, D)
        r_01 = view(stage_q, 3 * TT * D, 2, T)
        upb = view(stage_lora, 0, H)
        dna = view(stage_lora, H, HT, P)
        tanh_k = view(stage_lora, 0, T)
        ex_k = view(stage_lora, T, T)
        wkv = view(stage_lora, 2 * T, T)
        states = view(stage_lora, 3 * T, T)
        rbuf = [r_01[:, 0, :], r_01[:, 1, :], view(stage_lora, 2 * H, T)]
        sw1r = view(stage_sw, 0, DT, SHT * P)
        sw2r = view(stage_sw, T, SHT, D)
        gAT = view(stage_sw, 0, T)
        gBT = view(stage_sw, T, T)
        ups = sb("ups", [P, HT, D // BLOCK])
        dns = sb("dns", [P, DT, H // BLOCK])
        obuf = sb("obuf", [P, TT, D])
        upa = obuf[:, 0, :].rearrange("p (t r) -> p t r", t=DT)
        dnb, gamma_bc = obuf[:, 1, :], obuf[:, 3, :]
        gA = sb("gA", [P, TT, P])
        gB = sb("gB", [P, TT, P])
        shr = gA[:].rearrange("p t c -> p (t c)").rearrange("p (t d) -> p t d", t=DT)
        kvr = gB[:, 0:2, :].rearrange("p t c -> p (t c)")
        wor = gB[:, 2:4, :]
        gwr = sb("gwr", [P, DT, E])
        b2r = sb("b2r", [P, D])
        gate_bc = sb("gate_bc", [P, D])
        keep_bc = gate_bc
        gate_c = sb("gate_c", [P, 2 * DT])
        beta_bc = sb("beta_bc", [P, D])
        tdec = sb("tdec", [P, 2])
        mhalf = sb("mhalf", [P, TT])
        xin = sb("xin", [P, TT, D])
        x_hl = pair("x_or_x2T", [P, TT * D])
        x2T_hl = [p[:].rearrange("p (t n) -> p t n", t=DT) for p in x_hl]
        x_hl = [p[:].rearrange("p (t n) -> p t n", t=TT) for p in x_hl]
        xT_hl = pair("xT_or_zT", [P, DT, T])
        zT_hl = xT_hl
        mx = sb("mx", [P, DT])
        nmx = sb("nmx", [P, DT])
        esum = sb("esum", [P, DT])
        erec = sb("erec", [P, DT])
        prob = sb("prob", [P, DT, D])
        kvb = x2[:, 0, :]
        PT_hl = pair("PT", [P, DT, D])
        x1T_hl = pair("x1T", [P, DT, T])
        st_hl = PT_hl[0][:].rearrange("p t d -> p (t d)")
        x3 = [x3_0, x1]
        x3T_hl = [pair("x3T", [P, DT, T]), x1T_hl]
        logit = sb("logit", [P, TT, 2 * E])
        top = sb("top", [P, TT, 8])
        marked = sb("marked", [P, TT, 2 * E])
        chosen = sb("chosen", [P, TT, E])
        gexp = sb("gexp", [P, TT, E])
        gsum = sb("gsum", [P, TT])
        gates = sb("gates", [P, TT, E])
        gates_hi = sb("gates_hi", [P, TT, E], F32R)
        gAT_r = sb("gAT_r", [P, T], F32R)
        r_hi = [sb(f"r_hi{i}", [P, T], F32R) for i in range(RING)]
        r_lo = [sb(f"r_lo{i}", [P, T], F32R) for i in range(RING)]
        upb_parts, dnb_parts = [r_hi[0], r_hi[1]], r_lo[0][:, 0:D]
        upaT, dnaT = r_lo[0][:, D:2 * D], [r_hi[2], r_lo[2]]
        a_hi = r_lo[1][:, 0:(DT + HT) * R].rearrange("p (t r) -> p t r", r=R)
        stats = {n: sb(f"stats{n}", [P, TT, 6]) for n in (0, 1)}
        mv = {n: sb(f"mv{n}", [P, TT, 2]) for n in range(1, 6)}
        veps = {n: sb(f"veps{n}", [P, TT]) for n in (0, 1)}
        rstd = {n: sb(f"rstd{n}", [P, TT]) for n in range(1, 6)}

        ld_x = sem("ld_x")
        ld_up = sem("ld_up")
        ld_lora = sem("ld_lora")
        ld_dn = sem("ld_dn")
        ld_l1 = sem("ld_l1")
        ld_bc = sem("ld_bc")
        ld_moe = sem("ld_moe")
        saved = sem("saved")
        zeroed = sem("zeroed")
        id_ready = sem("id_ready")
        const_ready = sem("const_ready")
        fold_v = sem("fold_v")
        fold_a = sem("fold_a")
        a_parts = sem("a_parts")
        b_hi = sem("b_hi")
        b_lo = sem("b_lo")
        lora_t = sem("lora_t")
        lora_sb = sem("lora_sb")
        up_ps = sem("up_ps")
        up_hi = sem("up_hi")
        up_lo = sem("up_lo")
        dn_ps = sem("dn_ps")
        dn_hi = sem("dn_hi")
        dn_lo = sem("dn_lo")
        l1_ps = sem("l1_ps")
        l1_hi = sem("l1_hi")
        l1_lo = sem("l1_lo")
        wsplit = sem("wsplit")
        t_ps = {n: sem(f"ps_{n}") for n in ("xT", "x1T", "x2T", "zT", "x3T")}
        t_hi = {n: sem(f"hi_{n}") for n in t_ps}
        t_lo = {n: sem(f"lo_{n}") for n in t_ps}
        ln = {n: sem(f"ln{n}") for n in range(1, 6)}
        ln_eps = {n: sem(f"ln_eps{n}") for n in range(1, 6)}
        ln_r = {n: sem(f"ln_rstd{n}") for n in range(1, 6)}
        x_hi = sem("x_hi")
        x_parts = sem("x_parts")
        energy_ps = sem("energy_ps")
        soft_v = sem("soft_v")
        soft_e = sem("soft_e")
        PT_ps = sem("PT_ps")
        PT_hi = sem("PT_hi")
        PT_lo = sem("PT_lo")
        attn_ps = sem("attn_ps")
        res1 = sem("res1")
        hid_ps = sem("hid_ps")
        hid_r = sem("hid_r")
        hid_hi = sem("hid_hi")
        hid_lo = sem("hid_lo")
        ffn_ps = sem("ffn_ps")
        keep2 = sem("keep2")
        shift_ps = sem("shift_ps")
        kv_ps = sem("kv_ps")
        kv_act = sem("kv_act")
        kv_v = sem("kv_v")
        st_hi = sem("st_hi")
        out_ps = sem("out_ps")
        logit_ps = sem("logit_ps")
        gate_v = sem("gate_v")
        gate_e = sem("gate_e")
        gT_ps = sem("gT_ps")
        gT_sb = sem("gT_sb")
        g_bc = sem("g_bc")
        mhid_ps = sem("mhid_ps")
        mhid_r = sem("mhid_r")
        mhid_g = sem("mhid_g")
        mhid_hi = sem("mhid_hi")
        mhid_lo = sem("mhid_lo")
        moe_ps = sem("moe_ps")

        LN_OF = {1: (attn_ps, Mb), 2: (ffn_ps, Db), 3: (shift_ps, Mb), 4: (out_ps, Mb),
                 5: (moe_ps, Db)}
        N_SPLIT, PIECES = 2 * (4 + E), 6
        N_PICK, N_GATE, N_SOFT, N_KV = 13, 23, 5, 3

        def steps(text, base=0):
            for word in text.split():
                name, batch = word.split("@")
                name, *args = name.split(".")
                yield (name, base + int(batch), *map(int, args))

        def slot(b):
            return 1 if b == B - 1 else 0

        def f_slot(b, k):
            return (NU + k + (RING - HT % RING if b == 0 else 0)) % RING

        def m_slot(b, k):
            return (k + (NU if b == B - 1 else 0)) % RING

        def run(eng, ops):
            for s in steps(PLAN["start"]):
                if s[0] in ops:
                    ops[s[0]](*s[1:])
            for i in range(1, B - 1):
                for s in steps(PLAN["flow"], i):
                    if s[0] in ops and s[1] < B:
                        ops[s[0]](*s[1:])
            for s in steps(PLAN["end"]):
                if s[0] in ops:
                    ops[s[0]](*s[1:])

        block = ctx.enter_context(nc.Block())

        @block.sync
        def _(sp):
            def load_x(b):
                sp.dma_start(xin[:], x[b].rearrange("(t p) d -> p t d", p=P)).then_inc(ld_x, 16)

            load_x(0)
            sp.dma_start(upq, up_q.rearrange("(k p) d -> p k d", p=P)).then_inc(ld_up, 16)
            sp.dma_start(ups[:], up_scale.rearrange("(k p) c -> p k c", p=P)).then_inc(ld_up, 16)
            sp.wait_ge(zeroed, 1)
            sp.dma_start(upa[:, :, 0:R], up_a.rearrange("(t p) r -> p t r", p=P)).then_inc(ld_lora, 16)
            sp.dma_start(dna[:, :, 0:R], dn_a.rearrange("(k p) r -> p k r", p=P)).then_inc(ld_lora, 16)
            for n in range(3):
                sp.dma_start(upb[n * PART:n * PART + R, :], up_b).then_inc(ld_lora, 16)
                sp.dma_start(dnb[n * PART:n * PART + R, :], dn_b).then_inc(ld_lora, 16)
            sp.dma_start(dnq, dn_q.rearrange("(t p) h -> p t h", p=P)).then_inc(ld_dn, 16)
            sp.dma_start(dns[:], dn_scale.rearrange("(t p) c -> p t c", p=P)).then_inc(ld_dn, 16)
            sp.dma_start(bup_c[:], b_up.rearrange("(k p) -> p k", p=P),
                         allow_slow_non_contiguous=True).then_inc(ld_dn, 16)
            for dst, src in ((gate_bc, gate), (gamma_bc, ln_gamma), (beta_bc, ln_beta), (bdown_bc, b_down)):
                sp.dma_start(dst[:], src.rearrange("(a d) -> a d", a=1).to_broadcast((P, D))).then_inc(ld_bc, 16)
            sp.dma_start(gate_c[:, 0:DT], gate.rearrange("(t p) -> p t", p=P),
                         allow_slow_non_contiguous=True).then_inc(ld_bc, 16)
            sp.dma_start(shr[:], w_shift.rearrange("(t p) d -> p t d", p=P)).then_inc(ld_l1, 16)
            sp.dma_start(kvr[0:S, :], w_value).then_inc(ld_l1, 16)
            sp.dma_start(kvr[S:2 * S, :], w_key).then_inc(ld_l1, 16)
            sp.dma_start(wor[:, :, 0:S], w_output.rearrange("(t p) s -> p t s", p=P)).then_inc(ld_l1, 16)
            sp.dma_start(wor[:, :, S:2 * S], w_output.rearrange("(t p) s -> p t s", p=P)).then_inc(ld_l1, 16)
            sp.dma_start(tdec[0:S, 0:1], time_decay.rearrange("(s a) -> s a", a=1)).then_inc(ld_l1, 16)
            sp.dma_start(tdec[S:2 * S, 0:1], time_first.rearrange("(s a) -> s a", a=1)).then_inc(ld_l1, 16)
            sp.dma_start(w1r, w1.rearrange("e (t p) h -> p e t h", p=P)).then_inc(ld_moe, 16)
            sp.dma_start(w2r, w2.rearrange("e p d -> p e d")).then_inc(ld_moe, 16)
            sp.dma_start(sw1r, sw1.rearrange("(t p) h -> p t h", p=P)).then_inc(ld_moe, 16)
            sp.dma_start(sw2r, sw2.rearrange("(t p) d -> p t d", p=P)).then_inc(ld_moe, 16)
            sp.dma_start(b2r[1:1 + E, :], b2).then_inc(ld_moe, 16)
            sp.dma_start(b2r[1 + E:1 + 2 * E, :], b2).then_inc(ld_moe, 16)
            sp.dma_start(b2r[1 + 2 * E:2 + 2 * E, :], sb2.rearrange("(a d) -> a d", a=1)).then_inc(ld_moe, 16)
            sp.dma_start(b2r[PART + 1:PART + 1 + E, :], b2).then_inc(ld_moe, 16)
            sp.dma_start(b2r[PART + 1 + E:PART + 2 + E, :], sb2.rearrange("(a d) -> a d", a=1)).then_inc(ld_moe, 16)
            sp.dma_start(b1_c[:, 0:E], b1.rearrange("e p -> p e"),
                         allow_slow_non_contiguous=True).then_inc(ld_moe, 16)
            sp.dma_start(b1_c[:, E:NU], sb1.rearrange("(k p) -> p k", p=P),
                         allow_slow_non_contiguous=True).then_inc(ld_moe, 16)
            sp.dma_start(gwr[:], gate_w.rearrange("(t p) e -> p t e", p=P)).then_inc(ld_moe, 16)

            def save(b):
                for i in range(2):
                    sp.wait_ge(ln[5], b * LN_DONE + LN_AGGR + 2 * i + 2)
                    sp.dma_start(out[b, 2 * i * P:2 * (i + 1) * P].rearrange("(t p) d -> p t d", p=P),
                                 obuf[:, 2 * i:2 * i + 2, :]).then_inc(saved, 16)

            for b in range(1, B):
                sp.wait_ge(ln[1], (b - 1) * LN_DONE + LN_SUMS)
                load_x(b)
                if b >= 2:
                    save(b - 2)
            save(B - 2)
            save(B - 1)
            sp.wait_ge(saved, 2 * 16 * B)

        @block.gpsimd
        def _(pool):
            g = nc.gpsimd
            g.memset(ident[:], 0.0).then_inc(id_ready, 1)
            pool.wait_ge(id_ready, 1)
            g.affine_select(out=ident[:], in_=ident[:], compare_op=ALU.not_equal, fill=1.0, base=0,
                            pattern=[[-1, P]], channel_multiplier=1).then_inc(id_ready, 1)
            for zero in (upa, upb, dna, dnb, b2r[:]):
                op = g.memset(zero, 0.0)
            op.then_inc(zeroed, 1)
            g.memset(mhalf[:], -0.5).then_inc(const_ready, 1)
            g.memset(logit[:], FILLER).then_inc(const_ready, 1)

            def ln_aggr(b, n):
                if n == 1:
                    pool.wait_ge(const_ready, 3)
                pool.wait_ge(ln[n], b * LN_DONE + LN_AGGR)
                g.tensor_scalar(veps[n in (2, 5)][:], mv[n][:, :, 1], EPS, None, ALU.add).then_inc(ln_eps[n], 1)
                pool.wait_ge(ln_eps[n], b + 1)
                g.tensor_tensor(rstd[n][:], veps[n in (2, 5)][:], mhalf[:], ALU.pow).then_inc(ln_r[n], 1)

            def bias_row(b, i):
                pool.wait_ge(ld_bc, 16 * 5)
                if b == 0:
                    pool.wait_ge(dn_lo, 4)
                else:
                    pool.wait_ge(ln[2], (b - 1) * LN_DONE + LN_SUMS)
                pool.wait_ge(ln[1], b * LN_DONE + LN_AGGR + 2 * i + 2)
                for t in (2 * i, 2 * i + 1):
                    g.tensor_tensor(x1res[:, t, :], x1[:, t, :], bdown_bc[:], ALU.add).then_inc(res1, 1)

            def keep_row(b, i):
                pool.wait_ge(fold_a, 3)
                pool.wait_ge(fold_v, 8)
                pool.wait_ge(wsplit, N_SPLIT)
                pool.wait_ge(ln[2], b * LN_DONE + LN_AGGR + 2 * i + 2)
                for t in (2 * i, 2 * i + 1):
                    g.tensor_tensor(x2keep[:, t, :], x2[:, t, :], keep_bc[:], ALU.mult).then_inc(keep2, 1)

            parts = [(hl[0][at], raw[at], hl[1][at], raw[at], f32(hl[0][at])) for hl, raw, at in
                     [(gw_hl, gwr, slice(None)), (sw1_hl, sw1r, slice(None)), (sw2_hl, sw2r, slice(None))]
                     + [(hl, raw, (slice(None), slice(e, e + 2))) for e in range(0, E, 2) for hl, raw in
                        ((w1_hl, w1r), (w2_hl, w2r))]]
            low = slice(PART, 2 * PART)
            parts.insert(1, (b2_rows[:], b2r[:], b2_rows[low, :], b2r[low, :], f32(b2_rows[low, :])))

            def fold_moe(_, piece):
                pool.wait_ge(ld_moe, 16 * 12)
                for n in range(len(parts) * piece // PIECES, len(parts) * (piece + 1) // PIECES):
                    hi, raw, lo, raw_lo, less = parts[n]
                    g.tensor_copy(hi, raw).then_inc(wsplit, 1)
                    pool.wait_ge(wsplit, 2 * n + 1)
                    g.tensor_tensor(lo, raw_lo, less, ALU.subtract).then_inc(wsplit, 1)
                    if n == 1:
                        pool.wait_ge(wsplit, 2 * n + 2)

            def lora_parts(_):
                pool.wait_ge(ld_lora, 16 * 8)
                for n, (raw, hi) in enumerate(((upa, a_hi[:, 0:DT, :]), (dna, a_hi[:, DT:DT + HT, :]))):
                    g.tensor_copy(hi, raw[:, :, 0:R]).then_inc(a_parts, 1)
                    pool.wait_ge(a_parts, 4 * n + 1)
                    g.tensor_tensor(raw[:, :, 2 * PART:2 * PART + R], raw[:, :, 0:R], f32(hi),
                                    ALU.subtract).then_inc(a_parts, 1)
                    g.tensor_copy(raw[:, :, PART:PART + R], f32(hi)).then_inc(a_parts, 1)
                    pool.wait_ge(a_parts, 4 * n + 2)
                    g.tensor_copy(raw[:, :, 0:R], f32(hi)).then_inc(a_parts, 1)

            def fold_l1(_):
                pool.wait_ge(l1_ps, 2)
                g.memset(gA[:], 0.0).then_inc(const_ready, 1)
                pool.wait_ge(const_ready, 4)
                g.memset(gA[:, :, 1 + 2 * E:2 + 2 * E], 1.0).then_inc(const_ready, 1)
                g.memset(gA[:, :, PART + 1 + E:PART + 2 + E], 1.0).then_inc(const_ready, 1)
                g.memset(gB[:], 0.0).then_inc(const_ready, 1)

            def gT(b):
                pool.wait_ge(gT_sb, b * 3 + 1)
                for e in range(GB):
                    g.drain()
                    g.partition_broadcast(gbc[:, e, :], gAT[32 * e:32 * e + 1, :],
                                          channels=P).then_inc(g_bc, 1)
                g.drain()

            def eup(b, k):
                if k + GB < E:
                    pool.wait_ge(gT_sb, b * 3 + 2)
                    pool.wait_ge(mhid_g, b * E + k + 1)
                    g.drain()
                    g.partition_broadcast(gbc[:, k, :], gBT[32 * k:32 * k + 1, :],
                                          channels=P).then_inc(g_bc, 1)
                    g.drain()

            def ln_apply(b, n, i):
                if n == 1:
                    bias_row(b, i)
                if n == 2:
                    keep_row(b, i)

            run(pool, {"ln_aggr": ln_aggr, "ln_apply": ln_apply, "gT": gT,
                       "eup": eup, "fold_moe": fold_moe,
                       "lora_parts": lora_parts, "fold_l1": fold_l1})

        @block.scalar
        def _(act):
            a = nc.scalar
            def x_split(b, i):
                act.wait_ge(ld_x, b * 16 + 16)
                if i == 0 and b >= 2:
                    act.wait_ge(shift_ps, (b - 2) * 2 + 2)
                half = slice(2 * i, 2 * i + 2)
                a.activation(x_hl[0][:, half, :], xin[:, half, :], ACT.Copy).then_inc(x_hi, 1)

            def turned(name, hl, b, t):
                act.wait_ge(t_ps[name], b * DT + t + 1)
                a.activation(hl[0][:, t, :], Tb[t][:], ACT.Copy).then_inc(t_hi[name], 1)

            def softmax(b):
                act.wait_ge(soft_v, b * N_SOFT + 2)
                for i in range(DT):
                    a.activation(prob[:, i, :], Mb[0][:, i * D:(i + 1) * D], ACT.Exp, bias=nmx[:, i:i + 1],
                                 accum_out=esum[:, i:i + 1]).then_inc(soft_e, 1)

            def PT(b):
                act.wait_ge(PT_ps, b + 1)
                a.activation(PT_hl[0][:].rearrange("p t d -> p (t d)"), Mb[1][:], ACT.Copy).then_inc(PT_hi, 1)

            def lora_parts(_):
                act.wait_ge(ld_lora, 16 * 8)
                for i in range(2):
                    a.activation(upb_parts[i][:], upb[:, i * 512:(i + 1) * 512], ACT.Copy).then_inc(b_hi, 1)
                a.activation(dnb_parts, dnb, ACT.Copy).then_inc(b_hi, 1)

            def lora(_):
                act.wait_ge(lora_t, 1)
                a.activation(upaT, Db[1][:, 0:D], ACT.Copy).then_inc(lora_sb, 1)
                for i in range(2):
                    act.wait_ge(lora_t, 2 + i)
                    a.activation(dnaT[i][:], Ub[i][:], ACT.Copy).then_inc(lora_sb, 1)

            def fold_up(_, n):
                act.wait_ge(up_ps, n + 1)
                a.activation(up_hl[0][:, n // 2, (n % 2) * 512:(n % 2 + 1) * 512], (Db + Ub)[n][:],
                             ACT.Copy).then_inc(up_hi, 1)

            def fold_down(_, n):
                act.wait_ge(dn_ps, n + 1)
                a.activation(dn_hl[0][:, 2 * n:2 * n + 2, :].rearrange("p k d -> p (k d)"),
                             (Db + Ub)[n][:], ACT.Copy).then_inc(dn_hi, 1)

            def gate_consts(_):
                act.wait_ge(ld_bc, 16 * 5)
                a.activation(gate_bc[:], gate_bc[:], ACT.Tanh, scale=0.5).then_inc(fold_a, 1)
                a.activation(gate_c[:, DT:2 * DT], gate_c[:, 0:DT], ACT.Tanh, scale=0.5).then_inc(fold_a, 1)
                act.wait_ge(ld_l1, 16 * 7)
                a.activation(tdec[:, 1:2], tdec[:, 0:1], ACT.Exp).then_inc(fold_a, 1)

            def fold_l1(_):
                act.wait_ge(l1_ps, 1)
                a.activation(sh_hl[0][:].rearrange("p t d -> p (t d)"), Mb[0][:], ACT.Copy).then_inc(l1_hi, 1)
                act.wait_ge(l1_ps, 2)
                a.activation(kv_hl[0][:].rearrange("p t d -> p (t d)"), Mb[1][:, 0:D], ACT.Copy).then_inc(l1_hi, 1)
                a.activation(wo_hl[0][:], Mb[1][:, D:2 * D], ACT.Copy).then_inc(l1_hi, 1)

            def up(b, k):
                act.wait_ge(hid_ps, b * HT + k + 1)
                r = f_slot(b, k)
                a.activation(rbuf[r], Ub[k % 2][:], ACT.Relu, bias=bup_c[:, k:k + 1]).then_inc(hid_r, 1)
                act.wait_ge(hid_r, b * HT + k + 1)
                a.activation(r_hi[r][:], rbuf[r], ACT.Copy).then_inc(hid_hi, 1)

            def kv(b):
                act.wait_ge(kv_ps, b + 1)
                a.activation(tanh_k[S:2 * S, :], Mb[0][S:2 * S, :], ACT.Tanh, bias=kvc[S:2 * S, 1:2],
                             scale=0.5).then_inc(kv_act, 1)
                act.wait_ge(kv_act, b * 2 + 1)
                a.activation(ex_k[0:S, :], tanh_k[S:2 * S, :], ACT.Exp, bias=kvc[S:2 * S, 2:3],
                             scale=kvc[S:2 * S, 2:3]).then_inc(kv_act, 1)

            def states_hi(b):
                act.wait_ge(kv_v, b * N_KV + 2)
                a.activation(st_hl[0:S, :], states[0:S, :], ACT.Copy).then_inc(st_hi, 1)

            def gate_exp(b):
                act.wait_ge(gate_v, b * N_GATE + 7)
                a.activation(gexp[:], gexp[:], ACT.Exp).then_inc(gate_e, 1)

            def gT(b):
                act.wait_ge(gT_ps, b * 2 + 1)
                a.activation(gAT, Tb[0][:], ACT.Copy).then_inc(gT_sb, 1)
                act.wait_ge(gT_ps, b * 2 + 2)
                a.activation(gBT, Tb[1][:], ACT.Copy).then_inc(gT_sb, 1)
                a.activation(gAT_r[:], Tb[0][:], ACT.Copy).then_inc(gT_sb, 1)

            def eup(b, k):
                r = m_slot(b, k)
                act.wait_ge(mhid_ps, b * NU + k + 1)
                a.activation(rbuf[r], Ub[k % 2][:], ACT.Gelu, bias=b1_c[:, k:k + 1]).then_inc(mhid_r, 1)
                if k < E:
                    act.wait_ge(mhid_g, b * E + k + 1)
                else:
                    act.wait_ge(mhid_r, b * NU + k + 1)
                a.activation(r_hi[r][:], rbuf[r], ACT.Copy).then_inc(mhid_hi, 1)

            run(act, {
                "x_split": x_split,
                "xT": lambda b, t: turned("xT", xT_hl, b, t),
                "x1T": lambda b, t: turned("x1T", x1T_hl, b, t),
                "x2T": lambda b, t: turned("x2T", x2T_hl, b, t),
                "zT": lambda b, t: turned("zT", zT_hl, b, t),
                "x3T": lambda b, t: turned("x3T", x3T_hl[slot(b)], b, t), "softmax": softmax, "PT": PT,
                "lora_parts": lora_parts, "lora": lora, "fold_up": fold_up, "fold_down": fold_down,
                "gate_consts": gate_consts, "fold_l1": fold_l1, "up": up, "kv": kv, "states": states_hi,
                "gate_exp": gate_exp, "gT": gT, "eup": eup})

        @block.vector
        def _(dve):
            v = nc.vector
            v.memset(decay[:], 1.0).then_inc(const_ready, 1)

            def x_split(b, i):
                half = slice(2 * i, 2 * i + 2)
                dve.wait_ge(x_hi, b * 2 + i + 1)
                v.tensor_tensor(x_hl[1][:, half, :], xin[:, half, :], f32(x_hl[0][:, half, :]),
                                ALU.subtract).then_inc(x_parts, 1)

            def turned(name, hl, b, t):
                dve.wait_ge(t_hi[name], b * DT + t + 1)
                v.tensor_tensor(hl[1][:, t, :], Tb[t][:], f32(hl[0][:, t, :]), ALU.subtract).then_inc(t_lo[name], 1)

            def ln_sum(b, n, i):
                ready, banks = LN_OF[n]
                y = {1: x1, 2: x2, 3: z, 4: x3[slot(b)], 5: obuf}[n]
                res = {1: xin, 2: x1res, 3: x2keep, 4: x2, 5: x3[slot(b)]}[n]
                base = b * LN_DONE
                if n == 1 and b == 0:
                    dve.wait_ge(up_ps, 4)
                if n == 1 and b > 0:
                    dve.wait_ge(res1, (b - 1) * TT + TT)
                if n == 2:
                    dve.wait_ge(res1, b * TT + 2 * i + 2)
                if n == 3:
                    dve.wait_ge(keep2, b * TT + 2 * i + 2)
                if n == 5 and b > 0:
                    dve.wait_ge(saved, b * 2 * 16)
                dve.wait_ge(ready, b * 2 + i + 1)
                v.tensor_tensor(y[:, 2 * i:2 * i + 2, :].rearrange("p t d -> p (t d)"), banks[i][:],
                                res[:, 2 * i:2 * i + 2, :].rearrange("p t d -> p (t d)"),
                                ALU.add).then_inc(ln[n], 1)
                dve.wait_ge(ln[n], base + 3 * i + 1)
                for t in (2 * i, 2 * i + 1):
                    v.bn_stats(stats[n in (2, 5)][:, t, :], y[:, t, :]).then_inc(ln[n], 1)

            def ln_aggr(b, n):
                dve.wait_ge(ln[n], b * LN_DONE + LN_STATS)
                for t in range(TT):
                    v.bn_aggr(mv[n][:, t, :], stats[n in (2, 5)][:, t, :]).then_inc(ln[n], 1)

            def ln_apply(b, n, i):
                dst = {1: x1, 2: x2, 3: z, 4: x3[slot(b)], 5: obuf}[n]
                dve.wait_ge(ln_r[n], b + 1)
                for t in (2 * i, 2 * i + 1):
                    v.tensor_scalar(dst[:, t, :], dst[:, t, :], mv[n][:, t, 0:1], rstd[n][:, t:t + 1],
                                    ALU.subtract, ALU.mult).then_inc(ln[n], 1)

            def softmax(b):
                base = b * N_SOFT
                dve.wait_ge(energy_ps, b + 1)
                v.tensor_reduce(mx[:], Mb[0][:].rearrange("p (i j) -> p i j", i=DT), AX.X, ALU.max).then_inc(soft_v, 1)
                dve.wait_ge(soft_v, base + 1)
                v.tensor_scalar(nmx[:], mx[:], -1.0, None, ALU.mult).then_inc(soft_v, 1)

            def soft_scale(b):
                base = b * N_SOFT
                dve.wait_ge(soft_e, b * DT + DT)
                v.reciprocal(erec[:], esum[:]).then_inc(soft_v, 1)
                dve.wait_ge(soft_v, base + 3)
                for i in range(DT):
                    v.tensor_scalar(prob[:, i, :], prob[:, i, :], erec[:, i:i + 1], None, ALU.mult).then_inc(soft_v, 1)

            def PT(b):
                dve.wait_ge(PT_hi, b + 1)
                v.tensor_tensor(PT_hl[1][:].rearrange("p t d -> p (t d)"), Mb[1][:],
                                f32(PT_hl[0][:]).rearrange("p t d -> p (t d)"), ALU.subtract).then_inc(PT_lo, 1)

            def dequant(dst, q, scale, n):
                v.scalar_tensor_tensor(
                    out=dst.rearrange("p k (c j) -> p (k c) j", j=BLOCK),
                    in0=q.rearrange("p k (c j) -> p (k c) j", j=BLOCK), scalar=-7.5,
                    in1=scale[:].rearrange("p k (c a) -> p (k c) a", a=1).to_broadcast((P, n, BLOCK)),
                    op0=ALU.add, op1=ALU.mult).then_inc(fold_v, 1)

            def deq_up(_):
                dve.wait_ge(ld_up, 16 * 2)
                dequant(wq, upq, ups, HT * D // BLOCK)

            def deq_down(_):
                dve.wait_ge(ld_dn, 16 * 3)
                dequant(wqd, dnq, dns, DT * H // BLOCK)

            def lora_parts(_):
                rows = (upb[:, 0:512], upb_parts[0]), (upb[:, 512:1024], upb_parts[1]), (dnb, dnb_parts)
                for n, (raw, hl) in enumerate(rows):
                    dve.wait_ge(b_hi, n + 1)
                    v.tensor_tensor(hl[PART:2 * PART, :], raw[PART:2 * PART, :], f32(hl[PART:2 * PART, :]),
                                    ALU.subtract).then_inc(b_lo, 1)

            def fold_up(_, n):
                dst = (slice(None), n // 2, slice((n % 2) * 512, (n % 2 + 1) * 512))
                dve.wait_ge(up_hi, n + 1)
                v.tensor_tensor(up_hl[1][dst], (Db + Ub)[n][:], f32(up_hl[0][dst]), ALU.subtract).then_inc(up_lo, 1)

            def fold_down(_, n):
                dve.wait_ge(dn_hi, n + 1)
                v.tensor_tensor(dn_hl[1][:, 2 * n:2 * n + 2, :].rearrange("p k d -> p (k d)"), (Db + Ub)[n][:],
                                f32(dn_hl[0][:, 2 * n:2 * n + 2, :]).rearrange("p k d -> p (k d)"),
                                ALU.subtract).then_inc(dn_lo, 1)

            def gate_consts(_):
                dve.wait_ge(fold_a, 2)
                v.tensor_scalar(gate_c[:, 0:DT], gate_c[:, DT:2 * DT], 0.5, 0.5, ALU.mult, ALU.add).then_inc(fold_v, 1)
                v.tensor_scalar(keep_bc[:], gate_bc[:], -0.5, 0.5, ALU.mult, ALU.add).then_inc(fold_v, 1)
                dve.wait_ge(ld_l1, 16 * 7)
                dve.wait_ge(fold_v, 4)
                for t in range(DT):
                    v.tensor_scalar(shr[:, t, :], shr[:, t, :], gate_c[:, t:t + 1], None, ALU.mult).then_inc(fold_v, 1)
                dve.wait_ge(up_ps, 4)
                v.tensor_tensor(kvb, kvr[:], beta_bc[:], ALU.mult).then_inc(fold_v, 1)
                v.tensor_tensor(kvr[:], kvr[:], gamma_bc[:], ALU.mult).then_inc(fold_v, 1)
                dve.wait_ge(fold_v, 8)
                v.tensor_reduce(kvc[:, 0:1], kvb, AX.X, ALU.add).then_inc(fold_v, 1)
                dve.wait_ge(fold_v, 9)
                v.tensor_scalar(kvc[:, 1:2], kvc[:, 0:1], 0.5, None, ALU.mult).then_inc(fold_v, 1)
                dve.wait_ge(fold_a, 3)
                v.tensor_scalar(kvc[:, 2:3], tdec[:, 1:2], -0.5, None, ALU.mult).then_inc(fold_v, 1)
                dve.wait_ge(const_ready, 3)
                v.tensor_scalar(decay[0:S, :], decay[0:S, :], tdec[0:S, 1:2], None, ALU.mult).then_inc(fold_v, 1)

            def fold_l1(_):
                dve.wait_ge(l1_hi, 1)
                v.tensor_tensor(sh_hl[1][:].rearrange("p t d -> p (t d)"), Mb[0][:],
                                f32(sh_hl[0][:]).rearrange("p t d -> p (t d)"), ALU.subtract).then_inc(l1_lo, 1)
                dve.wait_ge(l1_hi, 3)
                v.tensor_tensor(kv_hl[1][:].rearrange("p t d -> p (t d)"), Mb[1][:, 0:D],
                                f32(kv_hl[0][:]).rearrange("p t d -> p (t d)"), ALU.subtract).then_inc(l1_lo, 1)
                v.tensor_tensor(wo_hl[1][:], Mb[1][:, D:2 * D], f32(wo_hl[0][:]), ALU.subtract).then_inc(l1_lo, 1)

            def up(b, k):
                dve.wait_ge(hid_hi, b * HT + k + 1)
                r = f_slot(b, k)
                v.tensor_tensor(r_lo[r][:], rbuf[r], f32(r_hi[r][:]), ALU.subtract).then_inc(hid_lo, 1)

            def recur(b):
                dve.wait_ge(kv_act, b * 2 + 2)
                dve.wait_ge(fold_v, 12)
                v.scalar_tensor_tensor(out=wkv[0:S, :], in0=Mb[0][0:S, :], scalar=kvc[0:S, 0:1],
                                       in1=ex_k[0:S, :], op0=ALU.add, op1=ALU.mult).then_inc(kv_v, 1)
                dve.wait_ge(kv_v, b * N_KV + 1)
                v.tensor_tensor_scan(states[0:S, :], decay[0:S, :], wkv[0:S, :], 0.0, ALU.mult, ALU.add).then_inc(kv_v, 1)

            def states_lo(b):
                dve.wait_ge(st_hi, b + 1)
                v.tensor_tensor(st_hl[S:2 * S, :], states[0:S, :], f32(st_hl[0:S, :]), ALU.subtract).then_inc(kv_v, 1)

            def gating(b):
                base = b * N_GATE
                dve.wait_ge(logit_ps, b + 1)
                dve.wait_ge(const_ready, 7)
                two = Mb[1][:, 0:TT * 2 * E].rearrange("p (t e) -> p t e", t=TT)
                v.tensor_copy(logit[:, :, 0:E], two[:, :, E:2 * E]).then_inc(gate_v, 1)
                dve.wait_ge(gate_v, base + 1)
                v.tensor_tensor(logit[:, :, 0:E], two[:, :, 0:E], logit[:, :, 0:E], ALU.add).then_inc(gate_v, 1)
                dve.wait_ge(gate_v, base + 2)
                for t in range(TT):
                    v.max(top[:, t, :], logit[:, t, :]).then_inc(gate_v, 1)
                dve.wait_ge(gate_v, base + 6)
                v.tensor_tensor(gexp[:], logit[:, :, 0:E], top[:, :, 0:1].to_broadcast((P, TT, E)),
                                ALU.subtract).then_inc(gate_v, 1)
                v.memset(top[:, :, 2:8], FILLER).then_inc(gate_v, 1)
                dve.wait_ge(gate_v, base + 8)
                for t in range(TT):
                    v.match_replace(marked[:, t, :], top[:, t, :], logit[:, t, :], TAKEN).then_inc(gate_v, 1)
                dve.wait_ge(gate_v, base + 12)
                v.tensor_scalar(chosen[:], marked[:, :, 0:E], TAKEN, None, ALU.is_equal).then_inc(gate_v, 1)

            def gate_rows(b):
                base = b * N_GATE + N_PICK
                dve.wait_ge(gate_e, b + 1)
                dve.wait_ge(gate_v, base)
                v.tensor_tensor(gates[:], gexp[:], chosen[:], ALU.mult).then_inc(gate_v, 1)
                dve.wait_ge(gate_v, base + 1)
                v.tensor_reduce(gsum[:], gates[:], AX.X, ALU.add).then_inc(gate_v, 1)
                dve.wait_ge(gate_v, base + 2)
                v.reciprocal(gsum[:], gsum[:]).then_inc(gate_v, 1)
                dve.wait_ge(gate_v, base + 3)
                v.tensor_tensor(gates[:], gates[:], gsum[:].rearrange("p (t a) -> p t a", a=1).to_broadcast((P, TT, E)),
                                ALU.mult).then_inc(gate_v, 1)
                dve.wait_ge(gate_v, base + 4)
                v.tensor_copy(gates_hi[:], gates[:]).then_inc(gate_v, 1)
                v.tensor_copy(gA[:].rearrange("p t (j c) -> p t j c", c=PART)[:, :, :, 0],
                              gates[:, :, 0:4]).then_inc(gate_v, 1)
                v.tensor_copy(gB[:].rearrange("p t (j c) -> p t j c", c=PART)[:, :, :, 0],
                              gates[:, :, 4:8]).then_inc(gate_v, 1)
                dve.wait_ge(gate_v, base + 7)
                v.tensor_copy(gA[:, :, 1:1 + E], f32(gates_hi[:])).then_inc(gate_v, 1)
                v.tensor_copy(gA[:, :, PART + 1:PART + 1 + E], f32(gates_hi[:])).then_inc(gate_v, 1)
                v.tensor_tensor(gA[:, :, 1 + E:1 + 2 * E], gates[:], f32(gates_hi[:]), ALU.subtract).then_inc(gate_v, 1)

            def eup(b, k):
                r = m_slot(b, k)
                if k < E:
                    dve.wait_ge(mhid_r, b * NU + k + 1)
                    dve.wait_ge(g_bc, b * E + k + 1)
                    v.tensor_tensor(rbuf[r], rbuf[r], gbc[:, k % GB, :], ALU.mult).then_inc(mhid_g, 1)
                dve.wait_ge(mhid_hi, b * NU + k + 1)
                v.tensor_tensor(r_lo[r][:], rbuf[r], f32(r_hi[r][:]), ALU.subtract).then_inc(mhid_lo, 1)

            run(dve, {
                "x_split": x_split,
                "xT": lambda b, t: turned("xT", xT_hl, b, t),
                "x1T": lambda b, t: turned("x1T", x1T_hl, b, t),
                "x2T": lambda b, t: turned("x2T", x2T_hl, b, t),
                "zT": lambda b, t: turned("zT", zT_hl, b, t),
                "x3T": lambda b, t: turned("x3T", x3T_hl[slot(b)], b, t), "softmax": softmax, "soft_scale": soft_scale,
                "PT": PT, "ln_sum": ln_sum, "ln_aggr": ln_aggr, "ln_apply": ln_apply,
                "lora_parts": lora_parts, "deq_up": deq_up, "deq_down": deq_down,
                "fold_up": fold_up, "fold_down": fold_down, "gate_consts": gate_consts,
                "fold_l1": fold_l1, "up": up, "wkv": recur, "states": states_lo,
                "gating": gating, "gate_rows": gate_rows, "eup": eup})

        @block.tensor
        def _(pe):
            mm = nc.tensor.matmul

            def three(dst, w_hl, m_hl, cols, rows, first, last):
                for i, (w, m) in enumerate(((0, 0), (0, 1), (1, 0))):
                    op = mm(dst, w_hl[w][cols], m_hl[m][rows], start=first and i == 0,
                            stop=last and i == 2, skip_group_check=True)
                return op

            def turn(src, name, after, b, t):
                for c in range(TT):
                    if t == 0 and after is not None:
                        pe.wait_ge(after, b * LN_DONE + LN_AGGR + c + 1)
                    op = nc.tensor.transpose(Tb[t][:, c * P:(c + 1) * P], src[:, c, t * P:(t + 1) * P], ident[:])
                op.then_inc(t_ps[name], 1)

            def xT(b, t):
                pe.wait_ge(id_ready, 2)
                pe.wait_ge(ld_x, b * 16 + 16)
                if b == 1:
                    pe.wait_ge(t_lo["x1T"], DT)
                if b >= 2:
                    pe.wait_ge(gT_sb, (b - 2) * 3 + 3)
                turn(xin, "xT", None, b, t)

            def energy(b, i):
                if b == 1:
                    pe.wait_ge(l1_lo, 3)
                for c in range(TT):
                    if i == 0 and c % 2 == 0:
                        pe.wait_ge(x_parts, b * 2 + c // 2 + 1)
                    op = three(Mb[0][:, i * D:(i + 1) * D], x_hl, x_hl, (slice(None), c, slice(i * P, (i + 1) * P)),
                               (slice(None), c, slice(None)), c == 0, c == TT - 1)
                if i == DT - 1:
                    op.then_inc(energy_ps, 1)

            def PT(b):
                pe.wait_ge(soft_v, b * N_SOFT + 5)
                for j in range(DT):
                    for i in range(DT):
                        op = nc.tensor.transpose(Mb[1][:, j * D + i * P:j * D + (i + 1) * P],
                                                 prob[:, i, j * P:(j + 1) * P], ident[:])
                op.then_inc(PT_ps, 1)

            def attn(b, i):
                pe.wait_ge(PT_lo, b + 1)
                pe.wait_ge(t_lo["xT"], b * DT + DT)
                for c in (2 * i, 2 * i + 1):
                    for j in range(DT):
                        op = three(tok(Mb, c), xT_hl, PT_hl, (slice(None), j, slice(c * P, (c + 1) * P)),
                                   (slice(None), j, slice(None)), j == 0, j == DT - 1)
                    if c % 2:
                        op.then_inc(attn_ps, 1)

            def lora(_):
                pe.wait_ge(id_ready, 2)
                pe.wait_ge(a_parts, 8)
                for t in range(DT):
                    op = nc.tensor.transpose(Db[1][:, t * P:(t + 1) * P], upa[:, t, :], ident[:])
                op.then_inc(lora_t, 1)
                for k in range(HT):
                    op = nc.tensor.transpose(Ub[k // 4][:, k % 4 * P:(k % 4 + 1) * P], dna[:, k, :], ident[:])
                    if k % 4 == 3:
                        op.then_inc(lora_t, 1)

            def fold_up(_, n):
                if n == 0:
                    pe.wait_ge(lora_sb, 3)
                    pe.wait_ge(b_lo, 3)
                    pe.wait_ge(fold_v, 1)
                t, half = n // 2, n % 2
                dst = (Db + Ub)[n]
                mm(dst[:], upaT[:, t * P:(t + 1) * P], upb_parts[half][:], start=True,
                   stop=False, skip_group_check=True)
                for k in range(4):
                    op = mm(dst[:, k * P:(k + 1) * P], wq[:, half * 4 + k, t * P:(t + 1) * P], ident[:],
                            start=False, stop=True, skip_group_check=True)
                op.then_inc(up_ps, 1)

            def fold_down(_, n):
                if n == 0:
                    pe.wait_ge(fold_v, 2)
                pe.wait_ge(up_lo, n + 1)
                dst = (Db + Ub)[n]
                for k in range(2):
                    cols = slice(k * D, (k + 1) * D)
                    mm(dst[:, cols], dnaT[n // 2][:, (2 * n + k) % 4 * P:((2 * n + k) % 4 + 1) * P], dnb_parts, start=k == 0,
                       stop=False, skip_group_check=True)
                for k in range(2):
                    for t in range(DT):
                        op = mm(dst[:, k * D + t * P:k * D + (t + 1) * P], wqd[:, t, (2 * n + k) * P:(2 * n + k + 1) * P],
                                ident[:], start=False, stop=True, skip_group_check=True)
                op.then_inc(dn_ps, 1)

            def fold_l1(_):
                pe.wait_ge(ln[1], LN_SUMS)
                pe.wait_ge(fold_v, 8)
                for t in range(DT):
                    for e in range(DT):
                        op = nc.tensor.transpose(Mb[0][:, t * D + e * P:t * D + (e + 1) * P],
                                                 shr[:, e, t * P:(t + 1) * P], ident[:])
                op.then_inc(l1_ps, 1)
                for t in range(DT):
                    nc.tensor.transpose(Mb[1][:, t * P:(t + 1) * P], kvr[:, t * P:(t + 1) * P], ident[:])
                for t in range(DT):
                    op = nc.tensor.transpose(Mb[1][:, D + t * P:D + (t + 1) * P], wor[:, t, :], ident[:])
                op.then_inc(l1_ps, 1)

            def x1T(b, t):
                if b >= 2 and t == 0:
                    pe.wait_ge(t_lo["x2T"], (b - 1) * DT + DT)
                turn(x1, "x1T", ln[1], b, t)

            def up(b, k):
                if k == 0:
                    pe.wait_ge(dn_lo, 4)
                    pe.wait_ge(t_lo["x1T"], b * DT + DT)
                if k >= 2:
                    pe.wait_ge(hid_r, b * HT + k - 1)
                elif b >= 2:
                    pe.wait_ge(mhid_r, (b - 2) * NU + NU - 1 + k)
                elif b == 1:
                    pe.wait_ge(hid_r, HT - 1 + k)
                for t in range(DT):
                    op = three(Ub[k % 2][:], up_hl, x1T_hl, (slice(None), t, slice(k * P, (k + 1) * P)),
                               (slice(None), t, slice(None)), t == 0, t == DT - 1)
                op.then_inc(hid_ps, 1)

            def down_of(k, r, hl, first, last):
                for c in range(TT):
                    op = three(tok(Db, c), (r_hi[r], r_lo[r]), hl, (slice(None), slice(c * P, (c + 1) * P)),
                               (slice(None), k if hl is not sw2_hl else k - E, slice(None)), first and c % 2 == 0, last)
                    if last and c % 2:
                        op.then_inc(moe_ps if hl is not dn_hl else ffn_ps, 1)

            def down(b, k):
                pe.wait_ge(hid_lo, b * HT + k + 1)
                if k == 0 and b >= 2:
                    pe.wait_ge(ln[5], (b - 2) * LN_DONE + LN_SUMS)
                elif k == 0 and b == 1:
                    pe.wait_ge(ln[2], LN_SUMS)
                down_of(k, f_slot(b, k), dn_hl, k == 0, k == HT - 1)

            def x2T(b, t):
                if b == 0:
                    pe.wait_ge(t_lo["x1T"], DT + DT)
                elif b < B - 1:
                    pe.wait_ge(t_lo["xT"], (b + 1) * DT + DT)
                else:
                    pe.wait_ge(gT_sb, (b - 1) * 3 + 3)
                turn(x2, "x2T", ln[2], b, t)

            def shift(b, i):
                pe.wait_ge(l1_lo, 3)
                pe.wait_ge(t_lo["x2T"], b * DT + DT)
                if b < B - 1:
                    pe.wait_ge(ln[1], (b + 1) * LN_DONE + 3 * i + 1)
                for c in (2 * i, 2 * i + 1):
                    s = (c + TT // 2) % TT
                    for t in range(DT):
                        op = three(tok(Mb, c), x2T_hl, sh_hl, (slice(None), t, slice(s * P, (s + 1) * P)),
                                   (slice(None), t, slice(None)), t == 0, t == DT - 1)
                    if c % 2:
                        op.then_inc(shift_ps, 1)

            def zT(b, t):
                turn(z, "zT", ln[3], b, t)

            def kv(b):
                pe.wait_ge(t_lo["zT"], b * DT + DT)
                for t in range(DT):
                    op = three(Mb[0][:], kv_hl, zT_hl, (slice(None), t, slice(None)), (slice(None), t, slice(None)),
                               t == 0, t == DT - 1)
                op.then_inc(kv_ps, 1)

            def outp(b):
                pe.wait_ge(kv_v, b * N_KV + 3)
                for c in range(TT):
                    for n in range(2):
                        op = mm(tok(Mb, c), st_hl[:, c * P:(c + 1) * P], wo_hl[n][:], start=n == 0, stop=n == 1,
                                skip_group_check=True)
                    if c % 2:
                        op.then_inc(out_ps, 1)

            def x3T(b, t):
                turn(x3[slot(b)], "x3T", ln[4], b, t)

            def logits(b):
                pe.wait_ge(wsplit, N_SPLIT)
                pe.wait_ge(t_lo["x3T"], b * DT + DT)
                for c in range(TT):
                    for t in range(DT):
                        at = (slice(None), t, slice(c * P, (c + 1) * P))
                        mm(Mb[1][:, 2 * c * E:2 * (c + 1) * E], x3T_hl[slot(b)][0][at], gw_parts[:, t, :],
                           start=t == 0, stop=False, skip_group_check=True)
                        op = mm(Mb[1][:, 2 * c * E:(2 * c + 1) * E], x3T_hl[slot(b)][1][at], gw_parts[:, t, 0:E],
                                start=False, stop=t == DT - 1, skip_group_check=True)
                op.then_inc(logit_ps, 1)

            def gT(b):
                pe.wait_ge(gate_v, b * N_GATE + N_GATE)
                for n, src in enumerate((gA, gB)):
                    for c in range(TT):
                        op = nc.tensor.transpose(Tb[n][:, c * P:(c + 1) * P], src[:, c, :], ident[:])
                    op.then_inc(gT_ps, 1)

            def eup(b, k):
                if k == 0:
                    pe.wait_ge(wsplit, N_SPLIT)
                if k >= 2:
                    pe.wait_ge(mhid_r, b * NU + k - 1)
                elif b == B - 1:
                    pe.wait_ge(mhid_r, (b - 1) * NU + NU - 1 + k)
                else:
                    pe.wait_ge(hid_r, (b + 1) * HT + HT - 1 + k)
                w, cols = (w1_hl, (slice(None), k)) if k < E else (sw1_hl, (slice(None),))
                for t in range(DT):
                    at = (*cols, t, slice(None)) if k < E else (slice(None), t, slice((k - E) * P, (k - E + 1) * P))
                    op = three(Ub[k % 2][:], w, x3T_hl[slot(b)], at, (slice(None), t, slice(None)), t == 0, t == DT - 1)
                op.then_inc(mhid_ps, 1)

            def gbias(b):
                pe.wait_ge(gT_sb, b * 3 + 3)
                if b == B - 1:
                    pe.wait_ge(ln[5], (b - 1) * LN_DONE + LN_SUMS)
                else:
                    pe.wait_ge(ln[2], (b + 1) * LN_DONE + LN_SUMS)
                for c in range(TT):
                    mm(tok(Db, c), gAT_r[:, c * P:(c + 1) * P], b2_rows[:], start=c % 2 == 0, stop=False,
                       skip_group_check=True)

            def edown(b, k):
                pe.wait_ge(mhid_lo, b * NU + k + 1)
                down_of(k, m_slot(b, k), w2_hl if k < E else sw2_hl, False, k == NU - 1)

            run(pe, {"xT": xT, "energy": energy, "PT": PT, "attn": attn, "lora": lora,
                     "fold_up": fold_up, "fold_down": fold_down,
                     "fold_l1": fold_l1, "x1T": x1T, "up": up, "down": down, "x2T": x2T, "shift": shift, "zT": zT,
                     "kv": kv, "outp": outp, "x3T": x3T, "logits": logits, "gT": gT, "eup": eup, "gbias": gbias,
                     "edown": edown})


_INS = ["L0_attn_x", "L0_ffn_w_up_q", "L0_ffn_w_up_scale", "L0_ffn_b_up", "L0_ffn_w_up_lora_a",
        "L0_ffn_w_up_lora_b", "L0_ffn_w_down_q", "L0_ffn_w_down_scale", "L0_ffn_b_down",
        "L0_ffn_w_down_lora_a", "L0_ffn_w_down_lora_b", "L1_attn_W_key", "L1_attn_W_value",
        "L1_attn_W_output", "L1_attn_W_shift", "L1_attn_gate", "L1_attn_time_decay",
        "L1_attn_time_first", "L1_attn_ln_gamma", "L1_attn_ln_beta", "L1_ffn_gate_w", "L1_ffn_w1",
        "L1_ffn_b1", "L1_ffn_w2", "L1_ffn_b2", "L1_ffn_shared_w1", "L1_ffn_shared_b1",
        "L1_ffn_shared_w2", "L1_ffn_shared_b2"]


def kernel(**inputs):
    import numpy as np
    import concourse.bacc as bacc
    from concourse.bass_utils import run_bass_kernel_spmd

    nc = bacc.Bacc("TRN2", target_bir_lowering=False, num_devices=1)
    arrays, args = {}, []
    for name in _INS:
        a = np.ascontiguousarray(inputs[name])
        arrays[f"in_{name}"] = a
        args.append(nc.dram_tensor(f"in_{name}", a.shape, mybir.dt.from_np(a.dtype), kind="ExternalInput").ap())
    shape = inputs["L0_attn_x"].shape
    args.append(nc.dram_tensor("out_x", shape, F32, kind="ExternalOutput").ap())
    post_ln_kernel(nc, *args)
    r = run_bass_kernel_spmd(nc, [arrays], core_ids=[0])
    return r.results[0]["out_x"]
```
